# Optimizing a Trainium2 kernel written in Bass

```python
import numpy as np
import jax
import jax.numpy as jnp

def _softmax(x, axis=-1):
    return jax.nn.softmax(x, axis=axis)

def _gelu(x):
    return jax.nn.gelu(x, approximate=True)

def _silu(x):
    return jax.nn.silu(x)

def _sigmoid(x):
    return jax.nn.sigmoid(x)

def _layernorm(x, axis=-1, eps=1e-05):
    m = jnp.mean(x, axis=axis, keepdims=True)
    v = jnp.var(x, axis=axis, keepdims=True)
    return (x - m) / jnp.sqrt(v + eps)

def _scatter_add(tgt, idx, src, axis=0):
    return tgt.at[idx].add(src)

def _segment_sum(src, seg, n):
    return jax.ops.segment_sum(src, seg, n)
kernel_name = 'mk_prb_d1_jaxref_r8_cbbb7c'

def setup_inputs(seed: int=0):
    np.random.seed(seed)
    _w = jnp.asarray

    def _L0_attn_setup():
        import jax, jax.numpy as jnp
        import numpy as np
        WINDOW = 4
        TOPK = 8
        key = jax.random.key(seed)
        ks = jax.random.split(key, 14)
        B, N, D = (4, 256, 128)
        s = 0.02
        w = lambda k_, shp: jax.random.normal(k_, shp, jnp.float32) * s
        return {'mu': jax.random.normal(ks[0], (B, N, D), jnp.float32), 'Wq': w(ks[1], (D, D)), 'bq': jnp.zeros((D,), jnp.float32), 'Wk': w(ks[2], (D, D)), 'bk': jnp.zeros((D,), jnp.float32), 'Wv': w(ks[3], (D, D)), 'bv': jnp.zeros((D,), jnp.float32), 'Wm1': w(ks[4], (2 * D, D)), 'bm1': jnp.zeros((D,), jnp.float32), 'Wm2': w(ks[5], (D, D)), 'bm2': jnp.zeros((D,), jnp.float32), 'Wo': w(ks[6], (2 * D, D)), 'bo': jnp.zeros((D,), jnp.float32)}
    _L0_attn_in = _L0_attn_setup()

    def _L0_ffn_setup():
        import jax, jax.numpy as jnp
        import numpy as np
        E = 8
        D = 128
        H = 256
        TOP_K = 2
        key = jax.random.key(seed)
        k_x, k_g, k_w1, k_w2 = jax.random.split(key, 4)
        B, S = (4, 256)
        inp = {'input': jax.random.normal(k_x, (B, S, D), dtype=jnp.float32), 'Wg': jax.random.normal(k_g, (D, E), dtype=jnp.float32) * 0.02, 'W1': jax.random.normal(k_w1, (E, D, H), dtype=jnp.float32) * 0.02, 'b1': jnp.zeros((E, H), dtype=jnp.float32), 'W2': jax.random.normal(k_w2, (E, H, D), dtype=jnp.float32) * 0.02, 'b2': jnp.zeros((E, D), dtype=jnp.float32)}
        return inp
    _L0_ffn_in = _L0_ffn_setup()
    _d = {'L0_attn_mu': _L0_attn_in['mu'], 'L0_attn_Wq': _L0_attn_in['Wq'], 'L0_attn_bq': _L0_attn_in['bq'], 'L0_attn_Wk': _L0_attn_in['Wk'], 'L0_attn_bk': _L0_attn_in['bk'], 'L0_attn_Wv': _L0_attn_in['Wv'], 'L0_attn_bv': _L0_attn_in['bv'], 'L0_attn_Wm1': _L0_attn_in['Wm1'], 'L0_attn_bm1': _L0_attn_in['bm1'], 'L0_attn_Wm2': _L0_attn_in['Wm2'], 'L0_attn_bm2': _L0_attn_in['bm2'], 'L0_attn_Wo': _L0_attn_in['Wo'], 'L0_attn_bo': _L0_attn_in['bo'], 'L0_ffn_Wg': _L0_ffn_in['Wg'], 'L0_ffn_W1': _L0_ffn_in['W1'], 'L0_ffn_b1': _L0_ffn_in['b1'], 'L0_ffn_W2': _L0_ffn_in['W2'], 'L0_ffn_b2': _L0_ffn_in['b2']}
    _x0 = _d['L0_attn_mu']
    _d['L0_attn_mu'] = jax.random.normal(jax.random.fold_in(jax.random.key(seed), 1), (32, 256, 128), dtype=_x0.dtype)
    del _x0
    return _d

def reference(L0_attn_mu, L0_attn_Wq, L0_attn_bq, L0_attn_Wk, L0_attn_bk, L0_attn_Wv, L0_attn_bv, L0_attn_Wm1, L0_attn_bm1, L0_attn_Wm2, L0_attn_bm2, L0_attn_Wo, L0_attn_bo, L0_ffn_Wg, L0_ffn_W1, L0_ffn_b1, L0_ffn_W2, L0_ffn_b2):

    def _L0_attn_ref(mu, Wq, bq, Wk, bk, Wv, bv, Wm1, bm1, Wm2, bm2, Wo, bo):
        import jax, jax.numpy as jnp
        import numpy as np
        WINDOW = 4
        TOPK = 8
        B, N, D = mu.shape
        padded = jnp.pad(mu, ((0, 0), (WINDOW, 0), (0, 0)))
        neighbors = jnp.stack([padded[:, WINDOW - w:WINDOW - w + N, :] for w in range(1, WINDOW + 1)], axis=2)
        self_exp = jnp.broadcast_to(mu[:, :, None, :], neighbors.shape)
        h = jnp.concatenate([self_exp, neighbors], axis=-1)
        h = jax.nn.silu(h @ Wm1 + bm1) @ Wm2 + bm2
        local_msgs = h.mean(axis=2)
        q = mu @ Wq + bq
        k = mu @ Wk + bk
        v = mu @ Wv + bv
        scores = jnp.einsum('bnd,bmd->bnm', q, k) / np.sqrt(D).astype(np.float32)
        causal_mask = jnp.triu(jnp.ones((N, N), dtype=bool), k=1)
        scores = jnp.where(causal_mask[None], -jnp.inf, scores)
        if N > TOPK:
            topk_v, topk_i = jax.lax.top_k(scores, TOPK)
            bi = jnp.arange(B)[:, None, None]
            ni = jnp.arange(N)[None, :, None]
            sparse = jnp.full_like(scores, -jnp.inf).at[bi, ni, topk_i].set(topk_v)
            attn = jax.nn.softmax(sparse, axis=-1)
        else:
            attn = jax.nn.softmax(scores, axis=-1)
        glob = jnp.einsum('bnm,bmd->bnd', attn, v)
        return jnp.concatenate([local_msgs, glob], axis=-1) @ Wo + bo

    def _L0_ffn_ref(input, Wg, W1, b1, W2, b2):
        import jax, jax.numpy as jnp
        import numpy as np
        E = 8
        D = 128
        H = 256
        TOP_K = 2
        logits = jnp.einsum('bsd,de->bse', input, Wg)
        probs = jax.nn.softmax(logits, axis=-1)
        top_vals, top_idx = jax.lax.top_k(probs, TOP_K)
        top_vals = top_vals / jnp.sum(top_vals, axis=-1, keepdims=True)
        onehot = jax.nn.one_hot(top_idx, E, dtype=input.dtype)
        mask = jnp.sum(onehot, axis=2)
        scores = jnp.sum(onehot * top_vals[..., None], axis=2)
        xm = input[None] * jnp.moveaxis(mask, -1, 0)[..., None]
        h = jnp.einsum('ebsd,edh->ebsh', xm, W1) + b1[:, None, None, :]
        h = jax.nn.relu(h)
        y = jnp.einsum('ebsh,ehd->ebsd', h, W2) + b2[:, None, None, :]
        out = jnp.sum(y * jnp.moveaxis(scores, -1, 0)[..., None], axis=0)
        return out
    x = L0_attn_mu
    xn = _layernorm(x, axis=-1)
    x = x + _L0_attn_ref(xn, L0_attn_Wq, L0_attn_bq, L0_attn_Wk, L0_attn_bk, L0_attn_Wv, L0_attn_bv, L0_attn_Wm1, L0_attn_bm1, L0_attn_Wm2, L0_attn_bm2, L0_attn_Wo, L0_attn_bo) + _L0_ffn_ref(xn, L0_ffn_Wg, L0_ffn_W1, L0_ffn_b1, L0_ffn_W2, L0_ffn_b2)
    return x

_drawn_inputs = setup_inputs


def setup_inputs(seed=0):
    import zlib

    import numpy as np

    out = dict(_drawn_inputs(seed))
    spreads = {'L0_attn_bq': (0.0, 0.59),
     'L0_attn_bk': (0.0, 0.8),
     'L0_attn_bv': (0.0, 0.415),
     'L0_attn_bm1': (0.0, 0.8),
     'L0_attn_bm2': (0.0, 0.416),
     'L0_attn_bo': (0.0, 0.1),
     'L0_ffn_b1': (0.0, 0.533),
     'L0_ffn_b2': (0.0, 0.1)}
    factors = {'L0_attn_Wq': 3.189,
     'L0_attn_Wk': 3.055,
     'L0_attn_Wv': 2.859,
     'L0_attn_Wm1': 8.0,
     'L0_attn_Wm2': 8.0}
    for name, (base, spread) in spreads.items():
        noise = np.random.default_rng([zlib.crc32(name.encode()), seed]).standard_normal(out[name].shape)
        drawn = base * np.exp(spread * noise) if base else spread * noise
        out[name] = jnp.asarray(drawn.astype(out[name].dtype))
    for name, factor in factors.items():
        out[name] = (out[name] * factor).astype(out[name].dtype)
    return out
```

```python
from contextlib import ExitStack

import concourse.bass as bass
from concourse import mybir

ALU = mybir.AluOpType
ACT = mybir.ActivationFunctionType
AX_X = mybir.AxisListType.X
F32 = mybir.dt.float32
BF16 = mybir.dt.bfloat16
U32 = mybir.dt.uint32

P = 128
TG = 4
W = 4
TOP = 8
EPS = 1e-5
MASKED = -1e30
TAKEN = -3e38
TAKEN_BELOW = -1e37


def program(nc, mu, Wq, bq, Wk, bk, Wv, bv, Wm1, bm1, Wm2, bm2, Wo, bo, Wg, W1, b1, W2, b2, out):
    B, N, D = mu.shape
    E, _, H = W1.shape
    T = B * N
    NT = T // P
    NG = NT // TG
    GT = TG * P
    GB = GT // N
    HC = H // P
    assert D == P and N == 2 * P and GB == 2 and H % P == 0 and E == 8
    SCALE = float(D) ** -0.5
    SW = N // P + 1

    x_dram = mu.rearrange("b (j p) d -> p (b j) d", p=P)
    out_dram = out.rearrange("b (j p) d -> p (b j) d", p=P)

    with ExitStack() as ctx:
        def sb(name, shape, dt=F32):
            return ctx.enter_context(nc.sbuf_tensor(name, shape, dt))

        def sem(name):
            return ctx.enter_context(nc.semaphore(name))

        x = sb("x", [P, NT, D])
        xnT = sb("xnT", [P, T])
        xt = sb("xt", [P, 2, GT])
        sc = sb("sc", [P, 2, TG, E])
        score = sb("score", [P, NT, E])
        wq, wk, wv, wm2 = (sb(n, [P, D]) for n in ("wq", "wk", "wv", "wm2"))
        wm1 = sb("wm1", [P, 2, D])
        wo = sb("wo", [P, 2, D])
        wT = sb("wT", [P, 4, D])
        wqk = sb("wqk", [P, D])
        wvo = sb("wvo", [P, D])
        wloc = sb("wloc", [P, D])
        wgate = sb("wgate", [P, E + 1])
        w1 = sb("w1", [P, E, H])
        w2 = sb("w2", [P, E, HC, D])
        b1c = sb("b1c", [P, E, HC])
        bcol = sb("bcol", [P, 5])
        brep = sb("brep", [P, 3, P])
        qbias = sb("qbias", [P, 1])
        qkb = sb("qkb", [P, 1])
        b2r = sb("b2r", [TG * E, D])
        bor = sb("bor", [TG * E, D])
        b2blk = sb("b2blk", [TG * E, TG, D])
        ident = sb("ident", [P, P])
        identb = sb("identb", [P, P], BF16)
        future = sb("future", [P, P], BF16)
        ones = sb("ones", [P, P])
        lane = sb("lane", [P, TG, E])
        power = sb("power", [P, 3, TG])
        scratch = sb("scratch", [P, 1])
        st = sb("st", [P, 2, TG, 6])
        mv = sb("mv", [P, 2, TG, 2])
        rstd = sb("rstd", [P, 2, TG])
        xn = sb("xn", [P, 2, TG, D])
        bsb = sb("bsb", [P, 2, GB, W + N])
        u = sb("u", [P, W, GB, N])
        th = sb("th", [P, W, GB, N])
        hsum = sb("hsum", [P, 2, GT])
        q = sb("q", [P, 2, GT])
        v = sb("v", [P, 2, TG, D])
        s = sb("s", [P, 2, GB, SW * P])
        rest = sb("rest", [P, GB, SW * P])
        e = sb("e", [P, GB, SW * P])
        pr = sb("pr", [P, 2, GB, SW * P])
        pT = sb("pT", [P, GB, SW * P])
        top = sb("top", [P, 2, TG, TOP])
        negm = sb("negm", [P, 2, TG])
        topd = sb("topd", [P, TG, TOP])
        tope = sb("tope", [P, TG, TOP])
        den = sb("den", [P, 2, TG])
        rden = sb("rden", [P, 2, TG])
        lg = sb("lg", [P, 2, TG, E + 1])
        cb = sb("cb", [P, 2, TG])
        gtop = sb("gtop", [P, 2, TG, 8])
        gidx = sb("gidx", [P, TG, 8], U32)
        gif = sb("gif", [P, TG, 2])
        hot = sb("hot", [P, 2, 2, TG, E])
        gd = sb("gd", [P, TG])
        ge = sb("ge", [P, 2, TG])
        gden = sb("gden", [P, TG])
        gs = sb("gs", [P, 2, TG])
        gw = sb("gw", [P, 2, TG, E])
        scT = sb("scT", [TG * E, P])
        hid = sb("hid", [P, 2, HC, GT])

        ps = [ctx.enter_context(nc.psum_tensor(f"ps{i}", [P, 512], F32)) for i in range(8)]
        psT, psA, psB, psQL, psVO = ps[0], ps[1], ps[2], ps[3], ps[4]
        psS = [ps[5], ps[6]]
        psG = ps[7]
        hbank, ybank = ps[0:4], ps[4:6]

        wload = sem("wload")
        xload = [sem("xload0"), sem("xload1")]
        const_ready = sem("const_ready")
        pe_setup = sem("pe_setup")
        setup_done = sem("setup_done")
        vec_own = sem("vec_own")
        pool_own = sem("pool_own")
        stats_ready = sem("stats_ready")
        rstd_ready = sem("rstd_ready")
        xn_ready = sem("xn_ready")
        xT_psum = sem("xT_psum")
        xT_ready = sem("xT_ready")
        gate_psum = sem("gate_psum")
        a_psum = sem("a_psum")
        b_psum = sem("b_psum")
        q_psum = sem("q_psum")
        v_psum = sem("v_psum")
        s_psum = sem("s_psum")
        pT_psum = sem("pT_psum")
        scT_psum = sem("scT_psum")
        loc_psum = sem("loc_psum")
        o_psum = sem("o_psum")
        b_ready = sem("b_ready")
        q_ready = sem("q_ready")
        v_ready = sem("v_ready")
        s_ready = sem("s_ready")
        e_ready = sem("e_ready")
        den_ready = sem("den_ready")
        ge_ready = sem("ge_ready")
        pT_ready = sem("pT_ready")
        scT_ready = sem("scT_ready")
        tanh_ready = sem("tanh_ready")
        gate_read = sem("gate_read")
        cb_ready = sem("cb_ready")
        gtop_ready = sem("gtop_ready")
        hot_ready = sem("hot_ready")
        gd_ready = sem("gd_ready")
        score_ready = sem("score_ready")
        u_ready = sem("u_ready")
        hsum_ready = sem("hsum_ready")
        top_ready = sem("top_ready")
        pr_ready = sem("pr_ready")
        out_read = sem("out_read")
        hid_psum = sem("hid_psum")
        pool_gate = sem("pool_gate")
        kept = sem("kept")
        var_ready = sem("var_ready")
        setup_own = sem("setup_own")
        topd_ready = sem("topd_ready")
        vec_top = sem("vec_top")
        vec_den = sem("vec_den")
        vec_idx = sem("vec_idx")
        vec_gif = sem("vec_gif")
        vec_bn = sem("vec_bn")
        vec_sum = sem("vec_sum")
        hid_ready = sem("hid_ready")
        y_psum = sem("y_psum")
        y_added = sem("y_added")
        stored = [sem("stored0"), sem("stored1")]

        block = ctx.enter_context(nc.Block())

        LAGS = 3

        def wait(eng, sm, n):
            if isinstance(n, int) and n <= 0:
                return
            eng.wait_ge(sm, n)

        def wait_small(eng, sm, n):
            wait(eng, sm, n)
            eng.memset(scratch[:, :], 0.0)

        def run_steps(eng, body):
            lo, hi = LAGS + 2, NG - 1
            for t in range(lo):
                body(t, t % 2)
            with eng.Fori(0, (hi - lo) // 2) as n:
                for k in range(2):
                    body(n * 2 + (lo + k), (lo + k) % 2)
            for t in range(hi, NG + LAGS):
                body(t, t % 2)

        def group(t, par, lag):
            if isinstance(t, int) and not 0 <= t - lag < NG:
                return None, None
            return t - lag, (par - lag) % 2

        def tiles(tensor, g):
            return tensor[:, bass.ds(g * TG, TG), :]

        def tile(tensor, g, j):
            return tensor[:, bass.ds(g * TG + j, 1), :].rearrange("p a d -> p (a d)")

        @block.sync
        def _(sp):
            def load(g, b):
                wait(sp, xload[b], 16 * (g // 2) if isinstance(g, int) else (g - b) * 8)
                sp.dma_start(tiles(x, g), tiles(x_dram, g)).then_inc(xload[b], 16)

            load(0, 0)
            for dst, src in ((wq, Wq), (wk, Wk), (wv, Wv), (wm2, Wm2)):
                sp.dma_start(dst[:, :], src).then_inc(wload, 16)
            sp.dma_start(wm1[:, :, :], Wm1.rearrange("(a p) d -> p a d", p=P)).then_inc(wload, 16)
            sp.dma_start(wo[:, :, :], Wo.rearrange("(a p) d -> p a d", p=P)).then_inc(wload, 16)
            sp.dma_start(wgate[:, 0:E], Wg).then_inc(wload, 16)
            for n, src in enumerate((bq, bk, bv, bm1, bm2)):
                sp.dma_start(bcol[:, n:n + 1], src.rearrange("(p a) -> p a", a=1)).then_inc(wload, 16)
            for n in range(TG):
                sp.dma_start(b2r[n * E:(n + 1) * E, :], b2).then_inc(wload, 16)
            sp.dma_start(bor[:, :], bo.rearrange("(a d) -> a d", a=1).to_broadcast([TG * E, D])).then_inc(wload, 16)
            load(1, 1)
            sp.dma_start(w1[:, :, :], W1.rearrange("e d h -> d e h")).then_inc(wload, 16)
            sp.dma_start(w2[:, :, :, :], W2.rearrange("e (c p) d -> p e c d", p=P)).then_inc(wload, 16)
            sp.dma_start(b1c[:, :, :], b1.rearrange("e (c p) -> p e c", p=P),
                         allow_slow_non_contiguous=True).then_inc(wload, 16)
            with sp.Fori(1, NG // 2) as n:
                for k in range(2):
                    load(n * 2 + k, k)

            def store(g, b):
                sp.wait_ge(y_added, (g + 1) * E)
                sp.dma_start(tiles(out_dram, g), tiles(x, g)).then_inc(stored[b], 16)

            store(0, 0)
            store(1, 1)
            with sp.Fori(1, NG // 2) as n:
                for k in range(2):
                    store(n * 2 + k, k)
            for sm in stored:
                sp.wait_ge(sm, 16 * (NG // 2))

        N_W = 4 + 3 + 5 + TG + 1
        N_WLOAD = N_W + 3

        @block.gpsimd
        def _(pool):
            own = 0

            def link(ins):
                nonlocal own
                own += 1
                ins.then_inc(pool_own, 1)
                pool.wait_ge(pool_own, own)

            link(pool.memset(ones[:, :], 1.0))
            pool.affine_select(out=ident[:, :], in_=ones[:, :], compare_op=ALU.is_equal, fill=0.0, base=0,
                               pattern=[[-1, P]], channel_multiplier=1).then_inc(const_ready, 1)
            link(pool.memset(lane[:, :, :], 0.0))
            link(pool.memset(identb[:, :], 1.0))
            link(pool.affine_select(out=identb[:, :], in_=identb[:, :], compare_op=ALU.is_equal, fill=0.0, base=0,
                                    pattern=[[-1, P]], channel_multiplier=1))
            link(pool.memset(future[:, :], 0.0))
            link(pool.affine_select(out=future[:, :], in_=future[:, :], compare_op=ALU.is_ge, fill=MASKED, base=0,
                                    pattern=[[-1, P]], channel_multiplier=1))
            link(pool.memset(power[:, 0, :], -0.5))
            link(pool.memset(power[:, 1, :], -1.0))
            link(pool.memset(power[:, 2, :], EPS))
            pool.iota(lane[:, :, :], [[0, TG], [1, E]], base=0, channel_multiplier=0,
                      allow_small_or_imprecise_dtypes=True).then_inc(const_ready, 1)
            pool.wait_ge(const_ready, 2)
            pool.wait_ge(setup_done, 1)
            last = None
            for n in range(TG):
                last = pool.tensor_copy(b2blk[:, n, :], b2r[:, :])
            link(last)
            link(pool.affine_select(out=b2blk[:, :, :], in_=b2blk[:, :, :], compare_op=ALU.is_ge, fill=0.0, base=0,
                                    pattern=[[-E, TG], [0, D]], channel_multiplier=1))
            pool.affine_select(out=b2blk[:, :, :], in_=b2blk[:, :, :], compare_op=ALU.is_ge, fill=0.0, base=E - 1,
                               pattern=[[E, TG], [0, D]], channel_multiplier=-1).then_inc(const_ready, 1)

            def gates(t, par):
                g, b = group(t, par, 2)
                if g is None:
                    return
                pool.wait_ge(gtop_ready, g + 1)
                pool.tensor_tensor(gd[:, :], gtop[:, b, :, 1], gtop[:, b, :, 0], ALU.subtract).then_inc(gd_ready, 1)
                pool.wait_ge(ge_ready, g + 1)
                n = g * 5
                pool.tensor_tensor(gden[:, :], ge[:, b, :], ones[:, 0:TG], ALU.add).then_inc(pool_gate, 1)
                pool.wait_ge(pool_gate, n + 1)
                pool.tensor_tensor(gs[:, 0, :], gden[:, :], power[:, 1, :], ALU.pow).then_inc(pool_gate, 1)
                pool.wait_ge(pool_gate, n + 2)
                pool.tensor_tensor(gs[:, 1, :], ge[:, b, :], gs[:, 0, :], ALU.mult).then_inc(pool_gate, 1)
                pool.wait_ge(pool_gate, n + 3)
                pool.wait_ge(hot_ready, g + 1)
                for k in range(2):
                    pool.tensor_tensor(gw[:, k, :, :], hot[:, b, k, :, :],
                                       gs[:, k, :].unsqueeze(2).to_broadcast([P, TG, E]), ALU.mult).then_inc(pool_gate, 1)
                pool.wait_ge(pool_gate, n + 5)
                wait(pool, scT_psum, g - 1)
                pool.tensor_tensor(sc[:, b, :, :], gw[:, 0, :, :], gw[:, 1, :, :], ALU.add).then_inc(score_ready, 1)
                pool.wait_ge(score_ready, g + 1)
                pool.tensor_copy(tiles(score, g), sc[:, b, :, :])
                pool.wait_ge(xT_ready, g + 1)
                pool.tensor_copy(xnT[:, bass.ds(g * GT, GT)], xt[:, b, :]).then_inc(kept, 1)

            def step(t, par):
                g, b = group(t, par, 0)
                if g is not None:
                    pool.wait_ge(stats_ready, g + 1)
                    pool.tensor_tensor(rstd[:, b, :], mv[:, b, :, 1], power[:, 2, :], ALU.add).then_inc(var_ready, 1)
                    pool.wait_ge(var_ready, g + 1)
                    pool.tensor_tensor(rstd[:, b, :], rstd[:, b, :], power[:, 0, :], ALU.pow).then_inc(rstd_ready, 1)
                gates(t, par)

            run_steps(pool, step)

        @block.tensor
        def _(pe):
            pe.wait_ge(const_ready, 1)
            pe.wait_ge(wload, 16 * N_WLOAD)
            for n, w in enumerate((wq, wk, wv, wm2)):
                last = pe.transpose(psT[:, n * P:(n + 1) * P], w[:, :], ident[:, :])
            last.then_inc(pe_setup, 1)
            pe.wait_ge(setup_own, 2)
            pe.matmul(psA[:, 0:D], wT[:, 0, :], wT[:, 1, :], start=True, stop=True)
            pe.matmul(psA[:, D:2 * D], wT[:, 2, :], wo[:, 1, :], start=True, stop=True)
            pe.matmul(psA[:, 2 * D:3 * D], wT[:, 3, :], wo[:, 0, :], start=True, stop=True)
            pe.matmul(psB[:, 0:1], wT[:, 1, :], bcol[:, 0:1], start=True, stop=True)
            pe.matmul(psB[:, 2:3], wT[:, 0, :], bcol[:, 1:2], start=True, stop=True)
            pe.matmul(psB[:, 4:5], brep[:, 0, :], bcol[:, 1:2], start=True, stop=True)
            pe.matmul(psB[0:TG * E, D:2 * D], brep[:, 1, 0:TG * E], wo[:, 1, :], start=True, stop=False)
            pe.matmul(psB[0:TG * E, D:2 * D], brep[:, 2, 0:TG * E], wo[:, 0, :], start=False,
                      stop=True).then_inc(pe_setup, 1)
            pe.wait_ge(setup_done, 1)
            pe.wait_ge(const_ready, 3)

            def step(t, par):
                g, b = group(t, par, 1)
                if g is not None:
                    pe.wait_ge(xn_ready, g + 1)
                    wait(pe, xT_ready, g)
                    for j in range(TG):
                        last = pe.transpose(psT[:, j * P:(j + 1) * P], xn[:, b, j, :], ident[:, :])
                    last.then_inc(xT_psum, 1)
                g, b = group(t, par, 2)
                if g is not None:
                    pe.wait_ge(xT_ready, g + 1)
                    wait(pe, scT_ready, g - 1)
                    wait(pe, gate_read, g)
                    for j in range(TG):
                        last = pe.matmul(psG[:, j * 16:j * 16 + E + 1], xt[:, b, j * P:(j + 1) * P], wgate[:, :],
                                         start=True, stop=True)
                    last.then_inc(gate_psum, 1)
                    wait(pe, b_ready, g)
                    pe.matmul(psB[:, :], wm1[:, 1, :], xt[:, b, :], start=True, stop=True).then_inc(b_psum, 1)
                    wait(pe, u_ready, g)
                    pe.matmul(psA[:, :], wm1[:, 0, :], xt[:, b, :], start=True, stop=True).then_inc(a_psum, 1)
                    wait(pe, out_read, 2 * (g - 1))
                    wait(pe, q_ready, g)
                    wait(pe, v_ready, g)
                    pe.matmul(psQL[:, :], wqk[:, :], xt[:, b, :], start=True, stop=True).then_inc(q_psum, 1)
                    for j in range(TG):
                        last = pe.matmul(psVO[:, j * P:(j + 1) * P], xt[:, b, j * P:(j + 1) * P], wvo[:, :],
                                         start=True, stop=True)
                    last.then_inc(v_psum, 1)
                g, b = group(t, par, 3)
                if g is not None:
                    pe.wait_ge(pr_ready, g + 1)
                    pe.wait_ge(s_ready, g + 1)
                    for h in range(GB):
                        for k in range(SW):
                            last = pe.transpose(psS[h][:, k * P:(k + 1) * P], pr[:, b, h, k * P:(k + 1) * P],
                                                ident[:, :])
                    last.then_inc(pT_psum, 1)
                    pe.wait_ge(score_ready, g + 1)
                    if not isinstance(t, int) or t - 2 < NG:
                        pe.wait_ge(gate_read, g + 2)
                    pe.transpose(psG[0:TG * E, P:2 * P], sc[:, b, :, :].rearrange("p j e -> p (j e)"), ident[:, :]).then_inc(scT_psum, 1)
                    pe.wait_ge(hsum_ready, g + 1)
                    pe.wait_ge(q_ready, (g + 2) if not isinstance(t, int) or t - 2 < NG else NG)
                    pe.wait_ge(scT_ready, g + 1)
                    pe.matmul(psQL[:, :], scT[:, :], b2blk[:, :, :], start=True, stop=False, skip_group_check=True)
                    for j in range(TG):
                        last = pe.matmul(psQL[:, j * P:(j + 1) * P], hsum[:, b, j * P:(j + 1) * P], wloc[:, :],
                                         start=False, stop=(j == TG - 1), skip_group_check=True)
                    last.then_inc(loc_psum, 1)
                    pe.wait_ge(pT_ready, g + 1)
                    pe.wait_ge(v_ready, (g + 2) if not isinstance(t, int) or t - 2 < NG else NG)
                    for h in range(GB):
                        o = psVO[:, 2 * h * P:(2 * h + 1) * P]
                        pe.matmul(o, pT[:, h, 0:P], v[:, b, 2 * h, :], start=True, stop=True)
                        o = psVO[:, (2 * h + 1) * P:(2 * h + 2) * P]
                        pe.matmul(o, pT[:, h, P:2 * P], v[:, b, 2 * h, :], start=True, stop=False)
                        last = pe.matmul(o, pT[:, h, 2 * P:3 * P], v[:, b, 2 * h + 1, :], start=False, stop=True)
                    last.then_inc(o_psum, 1)
                g, b = group(t, par, 2)
                if g is not None:
                    pe.wait_ge(q_ready, g + 1)
                    wait(pe, pT_ready, g)
                    for h in range(GB):
                        k0, k1 = (xt[:, b, (2 * h + k) * P:(2 * h + k + 1) * P] for k in range(2))
                        q0, q1 = (q[:, b, (2 * h + k) * P:(2 * h + k + 1) * P] for k in range(2))
                        pe.matmul(psS[h][:, 0:P], q0, k0, start=True, stop=False)
                        pe.matmul(psS[h][:, 0:P], identb[:, :], future[:, :], start=False, stop=True)
                        pe.matmul(psS[h][:, P:2 * P], q1, k0, start=True, stop=True)
                        pe.matmul(psS[h][:, 2 * P:3 * P], q1, k1, start=True, stop=False)
                        last = pe.matmul(psS[h][:, 2 * P:3 * P], identb[:, :], future[:, :], start=False, stop=True)
                    last.then_inc(s_psum, 1)

            run_steps(pe, step)

            pe.wait_ge(out_read, 2 * NG)
            pe.wait_ge(kept, NG)

            def experts(g):
                for ex in range(E):
                    k, r = g * E + ex, ex % 2
                    for c in range(HC):
                        wait(pe, hid_ready, (k - 2) * HC + c + 1)
                        pe.matmul(hbank[r * HC + c][:, :], w1[:, ex, c * P:(c + 1) * P], xnT[:, bass.ds(g * GT, GT)],
                                  start=True, stop=True).then_inc(hid_psum, 1)
                    pe.wait_ge(hid_ready, (k + 1) * HC)
                    wait(pe, y_added, k - 1)
                    for j in range(TG):
                        for c in range(HC):
                            last = pe.matmul(ybank[r][:, j * P:(j + 1) * P], hid[:, r, c, j * P:(j + 1) * P],
                                             w2[:, ex, c, :], start=(c == 0), stop=(c == HC - 1))
                    last.then_inc(y_psum, 1)

            experts(0)
            with pe.Fori(1, NG) as g:
                experts(g)

        @block.scalar
        def _(act):
            def step(t, par):
                g, b = group(t, par, 3)
                if g is not None:
                    for j in range(TG):
                        h, k = j // 2, j % 2
                        act.wait_ge(top_ready, TG * g + j + 1)
                        if j == 0:
                            wait(act, pr_ready, g)
                        at = slice(0, P) if k == 0 else slice(P, 3 * P)
                        nc.scalar.activation(e[:, h, at], s[:, b, h, at], ACT.Exp,
                                             bias=negm[:, b, j:j + 1]).then_inc(e_ready, 1)
                    act.wait_ge(topd_ready, g + 1)
                    nc.scalar.activation(tope[:, :, :], topd[:, :, :], ACT.Exp).then_inc(den_ready, 1)
                g, b = group(t, par, 1)
                if g is not None:
                    act.wait_ge(xT_psum, g + 1)
                    wait(act, s_psum, g - 1)
                    wait(act, kept, g - 1)
                    nc.scalar.copy(xt[:, b, :], psT[:, :]).then_inc(xT_ready, 1)
                g, b = group(t, par, 2)
                if g is not None:
                    act.wait_ge(b_psum, g + 1)
                    wait(act, u_ready, g - 1)
                    nc.scalar.activation(bsb[:, b, :, W:W + N], psB[:, :].rearrange("p (h n) -> p h n", h=GB),
                                         ACT.Identity, bias=bcol[:, 3:4]).then_inc(b_ready, 1)
                    act.wait_ge(q_psum, g + 1)
                    nc.scalar.activation(q[:, b, :], psQL[:, :], ACT.Identity, bias=qbias[:, :]).then_inc(q_ready, 1)
                    act.wait_ge(v_psum, g + 1)
                    nc.scalar.copy(v[:, b, :, :], psVO[:, :].rearrange("p (j d) -> p j d", j=TG)).then_inc(v_ready, 1)
                    act.wait_ge(gd_ready, g + 1)
                    nc.scalar.activation(ge[:, b, :], gd[:, :], ACT.Exp).then_inc(ge_ready, 1)
                g, b = group(t, par, 3)
                if g is not None:
                    act.wait_ge(pT_psum, g + 1)
                    wait(act, o_psum, g)
                    for h in range(GB):
                        last = nc.scalar.copy(pT[:, h, :], psS[h][:, 0:SW * P])
                    last.then_inc(pT_ready, 1)
                    act.wait_ge(scT_psum, g + 1)
                    wait(act, loc_psum, g)
                    nc.scalar.copy(scT[:, :], psG[0:TG * E, P:2 * P]).then_inc(scT_ready, 1)
                g, b = group(t, par, 2)
                if g is not None:
                    act.wait_ge(u_ready, g + 1)
                    wait(act, hsum_ready, g)
                    nc.scalar.activation(th[:, :, :, :], u[:, :, :, :], ACT.Tanh, scale=0.5).then_inc(tanh_ready, 1)
                    act.wait_ge(s_psum, g + 1)
                    act.wait_ge(cb_ready, g + 1)
                    wait(act, pr_ready, g - 1)
                    for j in range(TG):
                        h, k = j // 2, j % 2
                        at = slice(0, P) if k == 0 else slice(P, 3 * P)
                        last = nc.scalar.activation(s[:, b, h, at], psS[h][:, at], ACT.Identity, scale=SCALE,
                                                    bias=cb[:, b, j:j + 1])
                    last.then_inc(s_ready, 1)

            run_steps(act, step)

            def experts(g):
                for ex in range(E):
                    k, r = g * E + ex, ex % 2
                    wait(act, y_psum, k - 1)
                    for c in range(HC):
                        act.wait_ge(hid_psum, k * HC + c + 1)
                        nc.scalar.activation(hid[:, r, c, :], hbank[r * HC + c][:, :], ACT.Relu,
                                             bias=b1c[:, ex, c:c + 1]).then_inc(hid_ready, 1)

            experts(0)
            with act.Fori(1, NG) as g:
                experts(g)

        @block.vector
        def _(dve):
            dve.wait_ge(wload, 16 * N_WLOAD)
            dve.wait_ge(const_ready, 2)
            for n, col in enumerate((0, 2, 4)):
                last = dve.tensor_scalar(brep[:, n, :], ones[:, :], bcol[:, col:col + 1], None, ALU.mult)
            last.then_inc(setup_own, 1)
            for b in range(2):
                for h in range(GB):
                    dve.tensor_scalar(bsb[:, b, h, 0:W], ones[:, 0:W], bcol[:, 3:4], None, ALU.mult)
            dve.wait_ge(pe_setup, 1)
            dve.tensor_copy(wT[:, :, :], psT[:, :].rearrange("p (n d) -> p n d", n=4)).then_inc(setup_own, 1)
            dve.wait_ge(pe_setup, 2)
            dve.tensor_copy(wqk[:, :], psA[:, 0:D])
            dve.tensor_copy(wvo[:, :], psA[:, D:2 * D])
            dve.tensor_scalar(wloc[:, :], psA[:, 2 * D:3 * D], 0.5 / W, None, ALU.mult)
            dve.tensor_copy(qbias[:, :], psB[:, 0:1])
            dve.tensor_copy(wgate[:, E:E + 1], psB[:, 2:3])
            dve.tensor_scalar(qkb[:, :], psB[:, 4:5], SCALE, None, ALU.mult)
            dve.tensor_tensor(b2r[:, :], psB[0:TG * E, D:2 * D], b2r[:, :], ALU.add).then_inc(setup_own, 1)
            dve.wait_ge(setup_own, 3)
            dve.tensor_tensor(b2r[:, :], b2r[:, :], bor[:, :], ALU.add).then_inc(setup_done, 1)

            def blocks(j):
                return j // 2, (slice(0, P) if j % 2 == 0 else slice(P, 3 * P))

            def step(t, par):
                g, b = group(t, par, 3)
                if g is not None:
                    wait_small(dve, s_ready, g + 1)
                    for j in range(TG):
                        h, at = blocks(j)
                        last = dve.max(top[:, b, j, :], s[:, b, h, at])
                    last.then_inc(vec_top, 1)
                    dve.wait_ge(vec_top, g + 1)
                    for j in range(TG):
                        h, at = blocks(j)
                        dve.tensor_scalar(negm[:, b, j:j + 1], top[:, b, j, 0:1], -1.0, None,
                                          ALU.mult).then_inc(top_ready, 1)
                        dve.match_replace(rest[:, h, at], top[:, b, j, :], s[:, b, h, at], TAKEN)
                    dve.tensor_tensor(topd[:, :, :], top[:, b, :, :], top[:, b, :, 0:1].to_broadcast([P, TG, TOP]),
                                      ALU.subtract).then_inc(topd_ready, 1)
                    dve.wait_ge(topd_ready, g + 1)
                    for j in range(TG):
                        h, at = blocks(j)
                        dve.wait_ge(e_ready, TG * g + j + 1)
                        last = dve.scalar_tensor_tensor(out=pr[:, b, h, at], in0=rest[:, h, at], scalar=TAKEN_BELOW,
                                                        in1=e[:, h, at], op0=ALU.is_le, op1=ALU.mult)
                    last.then_inc(pr_ready, 1)
                    dve.wait_ge(den_ready, g + 1)
                    dve.tensor_reduce(den[:, b, :], tope[:, :, :], AX_X, ALU.add).then_inc(vec_den, 1)
                    dve.wait_ge(vec_den, g + 1)
                    dve.reciprocal(rden[:, b, :], den[:, b, :])
                g, b = group(t, par, 2)
                if g is not None:
                    dve.wait_ge(gate_psum, g + 1)
                    dve.tensor_copy(lg[:, b, :, :], psG[:, 0:TG * 16].rearrange("p (j e) -> p j e", j=TG)[:, :, 0:E + 1]
                                    ).then_inc(gate_read, 1)
                    dve.wait_ge(gate_read, g + 1)
                    dve.tensor_scalar(cb[:, b, :], lg[:, b, :, E], SCALE, qkb[:, :], ALU.mult, ALU.add).then_inc(cb_ready, 1)
                    wait_small(dve, cb_ready, g + 1)
                    for j in range(TG):
                        last = dve.max(gtop[:, b, j, :], lg[:, b, j, 0:E])
                    last.then_inc(gtop_ready, 1)
                    wait_small(dve, gtop_ready, g + 1)
                    for j in range(TG):
                        last = dve.max_index(gidx[:, j, :], gtop[:, b, j, :], lg[:, b, j, 0:E])
                    last.then_inc(vec_idx, 1)
                    dve.wait_ge(vec_idx, g + 1)
                    dve.tensor_copy(gif[:, :, :], gidx[:, :, 0:2]).then_inc(vec_gif, 1)
                    dve.wait_ge(a_psum, g + 1)
                    dve.wait_ge(b_ready, g + 1)
                    a = psA[:, :].rearrange("p (h n) -> p h n", h=GB)
                    for w in range(W):
                        last = dve.tensor_tensor(u[:, w, :, :], a, bsb[:, b, :, W - 1 - w:W - 1 - w + N], ALU.add)
                    last.then_inc(u_ready, 1)
                    dve.wait_ge(vec_gif, g + 1)
                    for k in range(2):
                        last = dve.tensor_tensor(hot[:, b, k, :, :], lane[:, :, :],
                                                 gif[:, :, k:k + 1].to_broadcast([P, TG, E]), ALU.is_equal)
                    last.then_inc(hot_ready, 1)
                g, b = group(t, par, 0)
                if g is not None:
                    dve.wait_ge(xload[b], 16 * (g // 2 + 1) if isinstance(g, int) else (g - b) * 8 + 16)
                    for j in range(TG):
                        last = dve.bn_stats(st[:, b, j, :], tile(x, g, j))
                    last.then_inc(vec_bn, 1)
                    wait_small(dve, vec_bn, g + 1)
                    for j in range(TG):
                        last = dve.bn_aggr(mv[:, b, j, :], st[:, b, j, :])
                    last.then_inc(stats_ready, 1)
                    dve.wait_ge(rstd_ready, g + 1)
                    wait(dve, xT_psum, g - 1)
                    for j in range(TG):
                        last = dve.tensor_scalar(xn[:, b, j, :], tile(x, g, j),
                                                 mv[:, b, j, 0:1], rstd[:, b, j:j + 1], ALU.subtract, ALU.mult)
                    last.then_inc(xn_ready, 1)
                g, b = group(t, par, 2)
                if g is not None:
                    dve.wait_ge(tanh_ready, g + 1)
                    dve.scalar_tensor_tensor(out=th[:, :, :, :].rearrange("p w h n -> p (w h n)"),
                                             in0=th[:, :, :, :].rearrange("p w h n -> p (w h n)"), scalar=1.0,
                                             in1=u[:, :, :, :].rearrange("p w h n -> p (w h n)"),
                                             op0=ALU.add, op1=ALU.mult).then_inc(vec_sum, 1)
                    dve.wait_ge(vec_sum, 2 * g + 1)
                    half = W // 2
                    dve.tensor_tensor(th[:, 0:half, :, :], th[:, 0:half, :, :], th[:, half:W, :, :],
                                      ALU.add).then_inc(vec_sum, 1)
                    dve.wait_ge(vec_sum, 2 * g + 2)
                    wait(dve, loc_psum, g - 1)
                    dve.tensor_tensor(hsum[:, b, :].rearrange("p (h n) -> p h n", h=GB), th[:, 0, :, :], th[:, 1, :, :],
                                      ALU.add).then_inc(hsum_ready, 1)
                g, b = group(t, par, 3)
                if g is not None:
                    dve.wait_ge(loc_psum, g + 1)
                    dve.tensor_tensor(tiles(x, g), psQL[:, :].rearrange("p (j d) -> p j d", j=TG), tiles(x, g),
                                      ALU.add).then_inc(out_read, 1)
                    dve.wait_ge(o_psum, g + 1)
                    dve.wait_ge(out_read, 2 * g + 1)
                    for j in range(TG):
                        xj = tile(x, g, j)
                        last = dve.scalar_tensor_tensor(out=xj, in0=psVO[:, j * P:(j + 1) * P],
                                                        scalar=rden[:, b, j:j + 1], in1=xj, op0=ALU.mult, op1=ALU.add)
                    last.then_inc(out_read, 1)

            run_steps(dve, step)

            dve.wait_ge(out_read, 2 * NG)
            dve.wait_ge(kept, NG)

            def experts(g):
                for ex in range(E):
                    k = g * E + ex
                    dve.wait_ge(y_psum, k + 1)
                    wait(dve, y_added, k)
                    for j in range(TG):
                        xj = tile(x, g, j)
                        last = dve.scalar_tensor_tensor(out=xj, in0=ybank[ex % 2][:, j * P:(j + 1) * P],
                                                        scalar=tile(score, g, j)[:, ex:ex + 1], in1=xj,
                                                        op0=ALU.mult, op1=ALU.add)
                    last.then_inc(y_added, 1)

            experts(0)
            with dve.Fori(1, NG) as g:
                experts(g)


_INS = ["L0_attn_mu", "L0_attn_Wq", "L0_attn_bq", "L0_attn_Wk", "L0_attn_bk", "L0_attn_Wv", "L0_attn_bv",
        "L0_attn_Wm1", "L0_attn_bm1", "L0_attn_Wm2", "L0_attn_bm2", "L0_attn_Wo", "L0_attn_bo",
        "L0_ffn_Wg", "L0_ffn_W1", "L0_ffn_b1", "L0_ffn_W2", "L0_ffn_b2"]


def kernel(**inputs):
    import numpy as _np
    import concourse.bacc as _bacc
    from concourse import mybir as _mybir
    from concourse.bass_utils import run_bass_kernel_spmd as _run

    nc = _bacc.Bacc("TRN2", target_bir_lowering=False, num_devices=1)
    arrays, args = {}, []
    for name in _INS:
        a = _np.ascontiguousarray(inputs[name])
        arrays[f"in_{name}"] = a
        args.append(nc.dram_tensor(f"in_{name}", a.shape, _mybir.dt.from_np(a.dtype), kind="ExternalInput").ap())
    shape = inputs["L0_attn_mu"].shape
    out = nc.dram_tensor("out_0", shape, _mybir.dt.float32, kind="ExternalOutput").ap()
    program(nc, *args, out)
    r = _run(nc, [arrays], core_ids=[0])
    return r.results[0]["out_0"]
```

```python
from contextlib import ExitStack

import concourse.bass as bass
from concourse import mybir

ALU = mybir.AluOpType
ACT = mybir.ActivationFunctionType
AX_X = mybir.AxisListType.X
F32 = mybir.dt.float32
BF16 = mybir.dt.bfloat16
U32 = mybir.dt.uint32

P = 128
TG = 4
W = 4
TOP = 8
K = 2
EPS = 1e-5
MASKED = -1e30
TAKEN = -3e38
TAKEN_BELOW = -1e37
JS = 2
UN = 8
XB = 4


def program(nc, mu, Wq, bq, Wk, bk, Wv, bv, Wm1, bm1, Wm2, bm2, Wo, bo, Wg, W1, b1, W2, b2, out):
    B, N, D = mu.shape
    E, _, H = W1.shape
    T = B * N
    NT = T // P
    NG = NT // TG
    GT = TG * P
    GB = GT // N
    HC = H // P
    SLOTS = JS * P
    NS = (K * T + E * (SLOTS - 1)) // SLOTS
    NS = -(-NS // UN) * UN
    LIST = T + SLOTS
    ROW = D + 2 * E
    NOWHERE = float(K * T)
    WX = H + HC * D + HC
    assert D == P and N == 2 * P and GB == 2 and HC == 2 and E == 8 and W == 4
    SCALE = float(D) ** -0.5
    SW = N // P + 1

    x_dram = mu.rearrange("b (j p) d -> p (b j) d", p=P)
    out_dram = out.rearrange("b (j p) d -> p (b j) d", p=P)
    lists = nc.dram_tensor("lists", [E * LIST + SLOTS, ROW], F32, kind="Internal").ap()
    results = nc.dram_tensor("results", [K * T, D], F32, kind="Internal").ap()
    results_by_tile = results.rearrange("(k t p) d -> p k t d", p=P, k=K)

    with ExitStack() as ctx:
        def sb(name, shape, dt=F32):
            return ctx.enter_context(nc.sbuf_tensor(name, shape, dt))

        def sem(name):
            return ctx.enter_context(nc.semaphore(name))

        x = sb("x", [P, NT, D])
        wq, wk, wv, wm2 = (sb(n, [P, D]) for n in ("wq", "wk", "wv", "wm2"))
        wm1 = sb("wm1", [P, 2, D])
        wo = sb("wo", [P, 2, D])
        wT = sb("wT", [P, 4, D])
        wqk = sb("wqk", [P, D])
        wvo = sb("wvo", [P, D])
        wloc = sb("wloc", [P, D])
        wgate = sb("wgate", [P, E + 1])
        wexp = sb("wexp", [P, E, WX])
        bcol = sb("bcol", [P, 5])
        brep = sb("brep", [P, 3, P])
        qbias = sb("qbias", [P, 1])
        qkb = sb("qkb", [P, 1])
        b2r = sb("b2r", [TG * E, D])
        bor = sb("bor", [TG * E, D])
        b2blk = sb("b2blk", [TG * E, TG, D])
        ident = sb("ident", [P, P])
        identb = sb("identb", [P, P], BF16)
        future = sb("future", [P, P], BF16)
        earlier = sb("earlier", [P, P], BF16)
        onesb = sb("onesb", [P, P], BF16)
        ones = sb("ones", [P, P])
        lane = sb("lane", [P, TG, E])
        power = sb("power", [P, 2, TG])
        second = sb("second", [P, TG, E])
        gstep = sb("gstep", [P, TG])
        tok = sb("tok", [P, TG])
        scratch = sb("scratch", [P, 1])
        idle = sb("idle", [P, 1])
        st = sb("st", [P, 2, TG, 6])
        mv = sb("mv", [P, 2, TG, 2])
        rstd = sb("rstd", [P, 2, TG])
        rows = sb("rows", [P, 2, TG, ROW])
        xt = sb("xt", [P, 2, GT])
        bsb = sb("bsb", [P, 2, GB, W + N])
        u = sb("u", [P, W, GB, N])
        th = sb("th", [P, W, GB, N])
        hsum = sb("hsum", [P, 2, GT])
        q = sb("q", [P, 2, GT])
        v = sb("v", [P, 2, TG, D])
        s = sb("s", [P, GB, SW * P])
        rest = sb("rest", [P, GB, SW * P])
        e = sb("e", [P, GB, SW * P])
        pr = sb("pr", [P, GB, SW * P])
        pT = sb("pT", [P, GB, SW * P])
        top = sb("top", [P, TG, TOP])
        negm = sb("negm", [P, TG])
        topd = sb("topd", [P, TG, TOP])
        tope = sb("tope", [P, TG, TOP])
        den = sb("den", [P, 2, TG])
        rden = sb("rden", [P, 2, TG])
        lg = sb("lg", [P, TG, E + 1])
        cb = sb("cb", [P, 2, TG])
        gtop = sb("gtop", [P, TG, 8])
        gidx = sb("gidx", [P, TG, 8], U32)
        gif = sb("gif", [P, TG, K])
        hot = sb("hot", [P, 2, K, TG, E])
        both = sb("both", [P, 2, TG, E], BF16)
        gd = sb("gd", [P, TG])
        gth = sb("gth", [P, TG])
        gs = sb("gs", [P, K, TG])
        gw = sb("gw", [P, K, TG, E])
        weight = sb("weight", [P, 2, TG, E])
        gdst = sb("gdst", [P, TG, E])
        base = sb("base", [P, E])
        place = sb("place", [P, TG, E])
        placed = sb("placed", [P, K, TG, E])
        slotf = sb("slotf", [P, K, TG])
        slot = sb("slot", [P, 2, K, TG], U32)
        scT = sb("scT", [TG * E, P])
        pad = sb("pad", [P, JS, ROW])
        lbase = sb("lbase", [P, E])
        cnt = sb("cnt", [P, E])
        cnti = sb("cnti", [P, E], U32)
        ntile = sb("ntile", [P, E])
        ends = sb("ends", [P, 4, E])
        begin = sb("begin", [P, E])
        kth = sb("kth", [P, E])
        chosen = sb("chosen", [P, 3, E])
        sched = sb("sched", [P, 2])
        schedi = sb("schedi", [1, 2, P], U32)
        basei = sb("basei", [P, E], U32)
        xg = sb("xg", [P, XB, JS, ROW])
        xgT = sb("xgT", [P, 2, SLOTS])
        wcur = sb("wcur", [P, 2, WX])
        hid = sb("hid", [P, 2, HC, SLOTS])
        gsc = sb("gsc", [P, XB, JS])
        gto = sb("gto", [P, XB, JS], U32)
        y = sb("y", [P, 2, JS, D])
        yin = sb("yin", [P, 4, K, TG, D])

        ps = [ctx.enter_context(nc.psum_tensor(f"ps{i}", [P, 512], F32)) for i in range(8)]
        psT, psA, psB, psQL, psVO = ps[0], ps[1], ps[2], ps[3], ps[4]
        psS = [ps[5], ps[6]]
        psG = ps[7]
        LOGITS, SCT, RANK, TOTAL = 0, P, 2 * P, 2 * P + TG * E
        psX, psH, psY = ps[0:2], ps[2:4], ps[4:6]

        wload = sem("wload")
        eload = sem("eload")
        xload = [sem("xload0"), sem("xload1")]
        const_ready = sem("const_ready")
        late_const = sem("late_const")
        pe_setup = sem("pe_setup")
        setup_own = sem("setup_own")
        setup_done = sem("setup_done")
        pool_own = sem("pool_own")
        stats_ready = sem("stats_ready")
        var_ready = sem("var_ready")
        rstd_ready = sem("rstd_ready")
        xn_ready = sem("xn_ready")
        xT_psum = sem("xT_psum")
        xT_ready = sem("xT_ready")
        gate_psum = sem("gate_psum")
        a_psum = sem("a_psum")
        b_psum = sem("b_psum")
        q_psum = sem("q_psum")
        v_psum = sem("v_psum")
        s_psum = sem("s_psum")
        pT_psum = sem("pT_psum")
        scT_psum = sem("scT_psum")
        rank_psum = sem("rank_psum")
        loc_psum = sem("loc_psum")
        o_psum = sem("o_psum")
        b_ready = sem("b_ready")
        q_ready = sem("q_ready")
        v_ready = sem("v_ready")
        s_ready = sem("s_ready")
        e_ready = sem("e_ready")
        tope_ready = sem("tope_ready")
        gth_ready = sem("gth_ready")
        pT_ready = sem("pT_ready")
        scT_ready = sem("scT_ready")
        tanh_ready = sem("tanh_ready")
        gate_read = sem("gate_read")
        cb_ready = sem("cb_ready")
        gtop_ready = sem("gtop_ready")
        gidx_ready = sem("gidx_ready")
        gif_ready = sem("gif_ready")
        hot_ready = sem("hot_ready")
        both_ready = sem("both_ready")
        gd_ready = sem("gd_ready")
        gs_ready = sem("gs_ready")
        place_ready = sem("place_ready")
        placed_ready = sem("placed_ready")
        slotf_ready = sem("slotf_ready")
        slot_ready = sem("slot_ready")
        gw_ready = sem("gw_ready")
        row_ready = sem("row_ready")
        tok_ready = sem("tok_ready")
        sent = [sem("sent0"), sem("sent1")]
        u_ready = sem("u_ready")
        prod_ready = sem("prod_ready")
        hsum_ready = sem("hsum_ready")
        bn_ready = sem("bn_ready")
        max_ready = sem("max_ready")
        negm_ready = sem("negm_ready")
        topd_ready = sem("topd_ready")
        pr_ready = sem("pr_ready")
        den_ready = sem("den_ready")
        rest_ready = sem("rest_ready")
        sum_ready = sem("sum_ready")
        rden_ready = sem("rden_ready")
        loc_read = sem("loc_read")
        out_read = sem("out_read")
        table_own = sem("table_own")
        table_psum = sem("table_psum")
        table_ready = sem("table_ready")
        padded = sem("padded")
        gathered = [sem(f"gathered{i}") for i in range(XB)]
        xgT_psum = sem("xgT_psum")
        xgT_ready = sem("xgT_ready")
        wcur_ready = sem("wcur_ready")
        gto_ready = sem("gto_ready")
        hid_psum = sem("hid_psum")
        hid_ready = sem("hid_ready")
        y_psum = sem("y_psum")
        y_ready = sem("y_ready")
        returned = [sem("returned0"), sem("returned1")]
        yload = [sem(f"yload{i}") for i in range(4)]
        y_added = sem("y_added")
        stored = sem("stored")
        idled = sem("idled")

        block = ctx.enter_context(nc.Block())

        LAGS = 3
        N_WLOAD = 4 + 1 + 5 + 1 + 1 + TG + 1
        TABLE_STEPS = 23

        def wait(eng, sm, n):
            if isinstance(n, int) and n <= 0:
                return
            eng.wait_ge(sm, n)

        def wait_small(eng, sm, n):
            wait(eng, sm, n)
            eng.memset(scratch[:, :], 0.0)

        def run_steps(eng, body):
            lo, hi = LAGS + 2, NG - 1
            for t in range(lo):
                body(t, t % 2)
            with eng.Fori(0, (hi - lo) // 2) as n:
                for k in range(2):
                    body(n * 2 + (lo + k), (lo + k) % 2)
            for t in range(hi, NG + LAGS):
                body(t, t % 2)

        def group(t, par, lag):
            if isinstance(t, int) and not 0 <= t - lag < NG:
                return None, None
            return t - lag, (par - lag) % 2

        def tiles(tensor, g):
            return tensor[:, bass.ds(g * TG, TG), :]

        def tile(tensor, g, j):
            return tensor[:, bass.ds(g * TG + j, 1), :].rearrange("p a d -> p (a d)")

        def halves(g, b, per_group):
            return (g // 2 + 1) * per_group if isinstance(g, int) else (g + (2 - b)) * (per_group // 2)

        def passes(n, r):
            return 16 * (n // XB + 1) if isinstance(n, int) else (n + (XB - r % XB)) * (16 // XB)

        def slot_tiles(eng, body, lead, lag):
            for k in range(-lead, UN):
                body(k)
            with eng.Fori(1, NS // UN - 1) as n:
                for k in range(UN):
                    body(n * UN + k, k)
            for k in range(NS - UN, NS + lag):
                body(k)

        @block.sync
        def _(sp):
            def load(g, b):
                wait(sp, xload[b], 16 * (g // 2) if isinstance(g, int) else (g - b) * 8)
                sp.dma_start(tiles(x, g), tiles(x_dram, g)).then_inc(xload[b], 16)

            load(0, 0)
            for dst, src in ((wq, Wq), (wk, Wk), (wv, Wv), (wm2, Wm2)):
                sp.dma_start(dst[:, :], src).then_inc(wload, 16)
            sp.dma_start(wo[:, :, :], Wo.rearrange("(a p) d -> p a d", p=P)).then_inc(wload, 16)
            for n, src in enumerate((bq, bk, bv, bm1, bm2)):
                sp.dma_start(bcol[:, n:n + 1], src.rearrange("(p a) -> p a", a=1)).then_inc(wload, 16)
            sp.dma_start(wm1[:, :, :], Wm1.rearrange("(a p) d -> p a d", p=P)).then_inc(wload, 16)
            sp.dma_start(wgate[:, 0:E], Wg).then_inc(wload, 16)
            for n in range(TG):
                sp.dma_start(b2r[n * E:(n + 1) * E, :], b2).then_inc(wload, 16)
            sp.dma_start(bor[:, :], bo.rearrange("(a d) -> a d", a=1).to_broadcast([TG * E, D])).then_inc(wload, 16)
            load(1, 1)
            sp.dma_start(wexp[:, :, 0:H], W1.rearrange("e d h -> d e h")).then_inc(eload, 16)
            for c in range(HC):
                sp.dma_start(wexp[:, :, H + c * D:H + (c + 1) * D],
                             W2[:, c * P:(c + 1) * P, :].rearrange("e p d -> p e d")).then_inc(eload, 16)
            for c in range(HC):
                sp.dma_start(wexp[:, :, H + HC * D + c:H + HC * D + c + 1],
                             b1[:, c * P:(c + 1) * P].rearrange("e (p a) -> p e a", a=1),
                             allow_slow_non_contiguous=True).then_inc(eload, 16)
            with sp.Fori(1, NG // 2) as n:
                for k in range(2):
                    load(n * 2 + k, k)

            sp.wait_ge(late_const, 2)
            sp.dma_start(lists[E * LIST:E * LIST + SLOTS, :].rearrange("(j p) d -> p j d", p=P),
                         pad[:, :, :]).then_inc(padded, 16)
            sp.wait_ge(table_ready, 1)
            starts = nc.values_load_multi_w_load_instructions(
                basei[0:1, :], engines=(mybir.EngineType.SP,), min_val=0, max_val=E * LIST - SLOTS,
                skip_runtime_bounds_check_because="a list holds at most T rows")[1]
            for start in starts:
                sp.dma_start(lists[bass.ds(start, SLOTS), :].rearrange("(j p) d -> p j d", p=P),
                             pad[:, :, :]).then_inc(padded, 16)
            for b in range(2):
                sp.wait_ge(sent[b], 16 * K * TG * NG // 2)
            sp.wait_ge(padded, 16 * (E + 1))
            sp.wait_ge(table_ready, 2)

            def fetch(k0, first):
                rows_of = nc.values_load_multi_w_load_instructions(
                    schedi[0:1, 1, bass.ds(k0, UN)], engines=(mybir.EngineType.SP,), min_val=0, max_val=E * LIST,
                    skip_runtime_bounds_check_because="the schedule names rows of the lists only")[1]
                for k in range(UN):
                    if not (first and k < XB):
                        sp.wait_ge(xgT_psum, k0 + k - XB + 1)
                        sp.wait_ge(gto_ready, k0 + k - XB + 1)
                    sp.dma_start(xg[:, k % XB, :, :],
                                 lists[bass.ds(rows_of[k], SLOTS), :].rearrange("(j p) d -> p j d", p=P)
                                 ).then_inc(gathered[k % XB], 16)

            fetch(0, True)
            with sp.Fori(1, NS // UN) as n:
                fetch(n * UN, False)

            for sm in returned:
                sp.wait_ge(sm, 16 * JS * NS // 2)

            def bring(g, b):
                wait(sp, y_added, g - 3)
                for k in range(K):
                    sp.dma_start(yin[:, b, k, :, :], results_by_tile[:, k, bass.ds(g * TG, TG), :]).then_inc(yload[b], 16)

            def store(g):
                sp.wait_ge(y_added, g + 1)
                sp.dma_start(tiles(out_dram, g), tiles(x, g)).then_inc(stored, 16)

            for g in range(4):
                bring(g, g % 4)
            with sp.Fori(1, NG // 4) as n:
                for k in range(4):
                    store(n * 4 + (k - 4))
                    bring(n * 4 + k, k)
            for g in range(NG - 4, NG):
                store(g)
            sp.wait_ge(stored, 16 * NG)

        @block.gpsimd
        def _(pool):
            own = 0

            def link(ins):
                nonlocal own
                own += 1
                ins.then_inc(pool_own, 1)
                pool.wait_ge(pool_own, own)

            link(pool.memset(ones[:, :], 1.0))
            pool.affine_select(out=ident[:, :], in_=ones[:, :], compare_op=ALU.is_equal, fill=0.0, base=0,
                               pattern=[[-1, P]], channel_multiplier=1).then_inc(const_ready, 1)
            pool.memset(power[:, 0, :], -0.5)
            pool.memset(power[:, 1, :], EPS).then_inc(const_ready, 1)
            link(pool.iota(lane[:, :, :], [[0, TG], [1, E]], base=0, channel_multiplier=0,
                           allow_small_or_imprecise_dtypes=True))
            link(pool.memset(onesb[:, :], 1.0))
            link(pool.affine_select(out=identb[:, :], in_=onesb[:, :], compare_op=ALU.is_equal, fill=0.0, base=0,
                                    pattern=[[-1, P]], channel_multiplier=1))
            link(pool.affine_select(out=earlier[:, :], in_=onesb[:, :], compare_op=ALU.is_ge, fill=0.0, base=-1,
                                    pattern=[[1, P]], channel_multiplier=-1))
            link(pool.memset(future[:, :], 0.0))
            link(pool.affine_select(out=future[:, :], in_=future[:, :], compare_op=ALU.is_ge, fill=MASKED, base=0,
                                    pattern=[[-1, P]], channel_multiplier=1))
            link(pool.memset(second[:, :, :], float(T)))
            link(pool.memset(gstep[:, :], float(GT)))
            link(pool.iota(tok[:, :], [[P, TG]], base=0, channel_multiplier=1,
                           allow_small_or_imprecise_dtypes=True))
            link(pool.iota(kth[:, :], [[0, E]], base=0, channel_multiplier=1,
                           allow_small_or_imprecise_dtypes=True))
            link(pool.iota(lbase[:, :], [[LIST, E]], base=0, channel_multiplier=0,
                           allow_small_or_imprecise_dtypes=True))
            pool.iota(base[:, :], [[LIST, E]], base=0, channel_multiplier=0,
                      allow_small_or_imprecise_dtypes=True).then_inc(const_ready, 1)
            pool.wait_ge(setup_done, 1)
            for n in range(TG):
                last = pool.tensor_copy(b2blk[:, n, :], b2r[:, :])
            link(last)
            link(pool.affine_select(out=b2blk[:, :, :], in_=b2blk[:, :, :], compare_op=ALU.is_ge, fill=0.0, base=0,
                                    pattern=[[-E, TG], [0, D]], channel_multiplier=1))
            pool.affine_select(out=b2blk[:, :, :], in_=b2blk[:, :, :], compare_op=ALU.is_ge, fill=0.0, base=E - 1,
                               pattern=[[E, TG], [0, D]], channel_multiplier=-1).then_inc(late_const, 1)
            link(pool.memset(pad[:, :, :], 0.0))
            pool.memset(pad[:, :, D + E:ROW], NOWHERE).then_inc(late_const, 1)

            def step(t, par):
                g, b = group(t, par, 0)
                if g is not None:
                    pool.wait_ge(stats_ready, g + 1)
                    wait(pool, xn_ready, g - 1)
                    pool.tensor_tensor(rstd[:, b, :], mv[:, b, :, 1], power[:, 1, :], ALU.add).then_inc(var_ready, 1)
                    pool.wait_ge(var_ready, g + 1)
                    pool.tensor_tensor(rstd[:, b, :], rstd[:, b, :], power[:, 0, :], ALU.pow).then_inc(rstd_ready, 1)
                g, b = group(t, par, 2)
                if g is not None:
                    pool.wait_ge(gs_ready, g + 1)
                    pool.tensor_tensor(gw[:, :, :, :], hot[:, b, :, :, :],
                                       gs[:, :, :].unsqueeze(3).to_broadcast([P, K, TG, E]),
                                       ALU.mult).then_inc(gw_ready, 1)
                    pool.tensor_tensor(gdst[:, :, :], hot[:, b, 1, :, :], second[:, :, :],
                                       ALU.mult).then_inc(gw_ready, 1)
                    wait(pool, tok_ready, g)
                    wait(pool, scT_psum, g - 1)
                    wait(pool, sent[b], halves(g - 2, b, 16 * K * TG) if not isinstance(g, int) or g >= 2 else 0)
                    pool.wait_ge(gw_ready, 2 * g + 2)
                    pool.tensor_tensor(weight[:, b, :, :], gw[:, 0, :, :], gw[:, 1, :, :], ALU.add)
                    pool.tensor_tensor(rows[:, b, :, D:D + E], gw[:, 0, :, :], gw[:, 1, :, :],
                                       ALU.add).then_inc(row_ready, 1)
                    pool.tensor_tensor(rows[:, b, :, D + E:ROW], gdst[:, :, :],
                                       tok[:, :].unsqueeze(2).to_broadcast([P, TG, E]), ALU.add).then_inc(row_ready, 1)
                    pool.wait_ge(row_ready, 2 * g + 2)
                    pool.wait_ge(slot_ready, g + 1)
                    pool.tensor_tensor(tok[:, :], tok[:, :], gstep[:, :], ALU.add).then_inc(tok_ready, 1)
                    for k in range(K):
                        for j in range(TG):
                            pool.indirect_dma_start(lists, bass.IndirectOffsetOnAxis(ap=slot[:, b, k, j:j + 1], axis=0),
                                                    rows[:, b, j, :], None).then_inc(sent[b], 16)

            run_steps(pool, step)

            def give(k, m):
                if not isinstance(k, int) or k:
                    pool.wait_ge(idled, k)
                pool.wait_ge(y_ready, k + 1)
                pool.tensor_tensor(idle[:, :], ones[:, 0:1], ones[:, 0:1], ALU.mult).then_inc(idled, 1)
                for j in range(JS):
                    pool.indirect_dma_start(results, bass.IndirectOffsetOnAxis(ap=gto[:, m % XB, j:j + 1], axis=0),
                                            y[:, m % 2, j, :], None, bounds_check=K * T - 1,
                                            oob_is_err=False).then_inc(returned[m % 2], 16)

            for m in range(UN):
                give(m, m)
            with pool.Fori(1, NS // UN) as n:
                for m in range(UN):
                    give(n * UN + m, m)

        @block.tensor
        def _(pe):
            pe.wait_ge(const_ready, 1)
            pe.wait_ge(wload, 16 * N_WLOAD)
            for n, w in enumerate((wq, wk, wv, wm2)):
                last = pe.transpose(psT[:, n * P:(n + 1) * P], w[:, :], ident[:, :])
            last.then_inc(pe_setup, 1)
            pe.wait_ge(setup_own, 2)
            pe.matmul(psA[:, 0:D], wT[:, 0, :], wT[:, 1, :], start=True, stop=True)
            pe.matmul(psA[:, D:2 * D], wT[:, 2, :], wo[:, 1, :], start=True, stop=True)
            pe.matmul(psA[:, 2 * D:3 * D], wT[:, 3, :], wo[:, 0, :], start=True, stop=True)
            pe.matmul(psB[:, 0:1], wT[:, 1, :], bcol[:, 0:1], start=True, stop=True)
            pe.matmul(psB[:, 2:3], wT[:, 0, :], bcol[:, 1:2], start=True, stop=True)
            pe.matmul(psB[:, 4:5], brep[:, 0, :], bcol[:, 1:2], start=True, stop=True)
            pe.matmul(psB[0:TG * E, D:2 * D], brep[:, 1, 0:TG * E], wo[:, 1, :], start=True, stop=False)
            pe.matmul(psB[0:TG * E, D:2 * D], brep[:, 2, 0:TG * E], wo[:, 0, :], start=False,
                      stop=True).then_inc(pe_setup, 1)
            pe.wait_ge(setup_done, 1)
            pe.wait_ge(const_ready, 3)

            def step(t, par):
                more = not isinstance(t, int) or t - 2 < NG
                g, b = group(t, par, 2)
                if g is not None:
                    pe.wait_ge(xT_ready, g + 1)
                    wait(pe, scT_ready, g - 1)
                    wait(pe, place_ready, 2 * g)
                    for j in range(TG):
                        last = pe.matmul(psG[:, LOGITS + j * 16:LOGITS + j * 16 + E + 1], xt[:, b, j * P:(j + 1) * P],
                                         wgate[:, :], start=True, stop=True)
                    last.then_inc(gate_psum, 1)
                    wait(pe, b_ready, g)
                    pe.matmul(psB[:, :], wm1[:, 1, :], xt[:, b, :], start=True, stop=True).then_inc(b_psum, 1)
                    wait(pe, u_ready, g)
                    pe.matmul(psA[:, :], wm1[:, 0, :], xt[:, b, :], start=True, stop=True).then_inc(a_psum, 1)
                    wait(pe, loc_read, g - 1)
                    wait(pe, q_ready, g)
                    pe.matmul(psQL[:, :], wqk[:, :], xt[:, b, :], start=True, stop=True).then_inc(q_psum, 1)
                g, b = group(t, par, 3)
                if g is not None:
                    pe.wait_ge(pr_ready, g + 1)
                    for h in range(GB):
                        for k in range(SW):
                            last = pe.transpose(psS[h][:, k * P:(k + 1) * P], pr[:, h, k * P:(k + 1) * P],
                                                ident[:, :])
                    last.then_inc(pT_psum, 1)
                    pe.wait_ge(row_ready, 2 * g + 2)
                    if more:
                        pe.wait_ge(gate_read, g + 2)
                    else:
                        pe.wait_ge(place_ready, 2 * NG)
                    pe.transpose(psG[0:TG * E, SCT:SCT + P], weight[:, b, :, :], ident[:, :]).then_inc(scT_psum, 1)
                g, b = group(t, par, 2)
                if g is not None:
                    wait(pe, out_read, g - 1)
                    wait(pe, v_ready, g)
                    for j in range(TG):
                        last = pe.matmul(psVO[:, j * P:(j + 1) * P], xt[:, b, j * P:(j + 1) * P], wvo[:, :],
                                         start=True, stop=True)
                    last.then_inc(v_psum, 1)
                g, b = group(t, par, 3)
                if g is not None:
                    pe.wait_ge(q_ready, g + 2 if more else NG)
                    pe.wait_ge(hsum_ready, g + 1)
                    for j in range(TG):
                        pe.matmul(psQL[:, j * P:(j + 1) * P], hsum[:, b, j * P:(j + 1) * P], wloc[:, :],
                                  start=(j == 0), stop=False, skip_group_check=True)
                    pe.wait_ge(late_const, 1)
                    pe.wait_ge(scT_ready, g + 1)
                    pe.matmul(psQL[:, :], scT[:, :], b2blk[:, :, :], start=False, stop=True,
                              skip_group_check=True).then_inc(loc_psum, 1)
                    pe.wait_ge(pT_ready, g + 1)
                    pe.wait_ge(v_ready, g + 2 if more else NG)
                    for h in range(GB):
                        o = psVO[:, 2 * h * P:(2 * h + 1) * P]
                        pe.matmul(o, pT[:, h, 0:P], v[:, b, 2 * h, :], start=True, stop=True)
                        o = psVO[:, (2 * h + 1) * P:(2 * h + 2) * P]
                        pe.matmul(o, pT[:, h, P:2 * P], v[:, b, 2 * h, :], start=True, stop=False)
                        last = pe.matmul(o, pT[:, h, 2 * P:3 * P], v[:, b, 2 * h + 1, :], start=False, stop=True)
                    last.then_inc(o_psum, 1)
                g, b = group(t, par, 1)
                if g is not None:
                    pe.wait_ge(xn_ready, g + 1)
                    wait(pe, xT_ready, g)
                    for j in range(TG):
                        last = pe.transpose(psT[:, j * P:(j + 1) * P], rows[:, b, j, 0:D], ident[:, :])
                    last.then_inc(xT_psum, 1)
                g, b = group(t, par, 2)
                if g is not None:
                    pe.wait_ge(both_ready, g + 1)
                    wait(pe, scT_ready, g)
                    rank = psG[:, RANK:RANK + TG * E]
                    pe.matmul(rank, earlier[:, :], both[:, b, :, :], start=True, stop=False)
                    for j in range(1, TG):
                        pe.matmul(psG[:, RANK + j * E:RANK + TG * E], onesb[:, :], both[:, b, 0:TG - j, :],
                                  start=False, stop=(j == TG - 1))
                    for j in range(TG):
                        last = pe.matmul(psG[:, TOTAL:TOTAL + E], onesb[:, :], both[:, b, j, :],
                                         start=(j == 0), stop=(j == TG - 1))
                    last.then_inc(rank_psum, 1)
                    pe.wait_ge(q_ready, g + 1)
                    wait(pe, pT_ready, g)
                    wait(pe, s_ready, g)
                    for h in range(GB):
                        k0, k1 = (xt[:, b, (2 * h + k) * P:(2 * h + k + 1) * P] for k in range(2))
                        q0, q1 = (q[:, b, (2 * h + k) * P:(2 * h + k + 1) * P] for k in range(2))
                        pe.matmul(psS[h][:, 0:P], q0, k0, start=True, stop=False)
                        pe.matmul(psS[h][:, 0:P], identb[:, :], future[:, :], start=False, stop=True)
                        pe.matmul(psS[h][:, P:2 * P], q1, k0, start=True, stop=True)
                        pe.matmul(psS[h][:, 2 * P:3 * P], q1, k1, start=True, stop=False)
                        last = pe.matmul(psS[h][:, 2 * P:3 * P], identb[:, :], future[:, :], start=False, stop=True)
                    last.then_inc(s_psum, 1)
                if isinstance(t, int) and t == NG + 1:
                    pe.wait_ge(table_own, TABLE_STEPS)
                    pe.wait_ge(place_ready, 2 * NG)
                    for n in range(2):
                        last = pe.transpose(psG[0:1, n * P:(n + 1) * P], sched[:, n:n + 1], ident[:, :])
                    last.then_inc(table_psum, 1)

            run_steps(pe, step)

            pe.wait_ge(out_read, NG)
            pe.wait_ge(xT_ready, NG)

            def tile_step(k, m=None):
                m = k % UN if m is None else m
                inside = lambda n: not isinstance(n, int) or 0 <= n < NS
                n, r = k + 1, (m + 1) % UN
                if inside(n):
                    pe.wait_ge(gathered[r % XB], passes(n, r))
                    wait(pe, xgT_ready, n - 1)
                    for j in range(JS):
                        last = pe.transpose(psX[r % 2][:, j * P:(j + 1) * P], xg[:, r % XB, j, 0:D], ident[:, :])
                    last.then_inc(xgT_psum, 1)
                n, r = k, m
                if inside(n):
                    pe.wait_ge(xgT_ready, n + 1)
                    pe.wait_ge(wcur_ready, n + 1)
                    wait(pe, hid_ready, HC * (n - 1))
                    for c in range(HC):
                        last = pe.matmul(psH[r % 2][:, c * SLOTS:(c + 1) * SLOTS], wcur[:, r % 2, c * P:(c + 1) * P],
                                         xgT[:, r % 2, :], start=True, stop=True)
                    last.then_inc(hid_psum, 1)
                n, r = k - 1, (m - 1) % UN
                if inside(n):
                    pe.wait_ge(hid_ready, HC * (n + 1))
                    wait(pe, y_ready, n - 1)
                    for j in range(JS):
                        for c in range(HC):
                            last = pe.matmul(psY[r % 2][:, j * P:(j + 1) * P], hid[:, r % 2, c, j * P:(j + 1) * P],
                                             wcur[:, r % 2, H + c * D:H + (c + 1) * D], start=(c == 0),
                                             stop=(c == HC - 1))
                    last.then_inc(y_psum, 1)

            slot_tiles(pe, tile_step, 1, 1)

        @block.scalar
        def _(act):
            def step(t, par):
                g, b = group(t, par, 2)
                if g is not None:
                    act.wait_ge(b_psum, g + 1)
                    act.wait_ge(setup_done, 1)
                    wait(act, u_ready, g - 1)
                    nc.scalar.activation(bsb[:, b, :, W:W + N], psB[:, :].rearrange("p (h n) -> p h n", h=GB),
                                         ACT.Identity, bias=bcol[:, 3:4]).then_inc(b_ready, 1)
                    act.wait_ge(q_psum, g + 1)
                    wait(act, s_psum, g - 1)
                    nc.scalar.activation(q[:, b, :], psQL[:, :], ACT.Identity, bias=qbias[:, :]).then_inc(q_ready, 1)
                g, b = group(t, par, 3)
                if g is not None:
                    act.wait_ge(pT_psum, g + 1)
                    wait(act, o_psum, g)
                    for h in range(GB):
                        last = nc.scalar.copy(pT[:, h, :], psS[h][:, 0:SW * P])
                    last.then_inc(pT_ready, 1)
                    act.wait_ge(scT_psum, g + 1)
                    wait(act, loc_psum, g)
                    nc.scalar.copy(scT[:, :], psG[0:TG * E, SCT:SCT + P]).then_inc(scT_ready, 1)
                g, b = group(t, par, 2)
                if g is not None:
                    act.wait_ge(v_psum, g + 1)
                    wait(act, o_psum, g - 1)
                    nc.scalar.copy(v[:, b, :, :], psVO[:, :].rearrange("p (j d) -> p j d", j=TG)).then_inc(v_ready, 1)
                    act.wait_ge(u_ready, g + 1)
                    wait(act, hsum_ready, g)
                    nc.scalar.activation(th[:, :, :, :], u[:, :, :, :], ACT.Tanh, scale=0.5).then_inc(tanh_ready, 1)
                    act.wait_ge(gd_ready, g + 1)
                    nc.scalar.activation(gth[:, :], gd[:, :], ACT.Tanh, scale=0.5).then_inc(gth_ready, 1)
                g, b = group(t, par, 1)
                if g is not None:
                    act.wait_ge(xT_psum, g + 1)
                    wait(act, s_psum, g - 1)
                    nc.scalar.copy(xt[:, b, :], psT[:, :]).then_inc(xT_ready, 1)
                g, b = group(t, par, 2)
                if g is not None:
                    act.wait_ge(s_psum, g + 1)
                    act.wait_ge(cb_ready, g + 1)
                    wait(act, pr_ready, g)
                    for j in range(TG):
                        h, k = j // 2, j % 2
                        at = slice(0, P) if k == 0 else slice(P, 3 * P)
                        last = nc.scalar.activation(s[:, h, at], psS[h][:, at], ACT.Identity, scale=SCALE,
                                                    bias=cb[:, b, j:j + 1])
                    last.then_inc(s_ready, 1)
                    act.wait_ge(negm_ready, g + 1)
                    for j in range(TG):
                        h, k = j // 2, j % 2
                        at = slice(0, P) if k == 0 else slice(P, 3 * P)
                        last = nc.scalar.activation(e[:, h, at], s[:, h, at], ACT.Exp, bias=negm[:, j:j + 1])
                    last.then_inc(e_ready, 1)
                    act.wait_ge(topd_ready, g + 1)
                    nc.scalar.activation(tope[:, :, :], topd[:, :, :], ACT.Exp).then_inc(tope_ready, 1)

            run_steps(act, step)

            def tile_step(k, m=None):
                m = k % UN if m is None else m
                inside = lambda n: not isinstance(n, int) or 0 <= n < NS
                n, r = k + 1, (m + 1) % UN
                if inside(n):
                    act.wait_ge(xgT_psum, n + 1)
                    wait(act, hid_psum, n - 1)
                    nc.scalar.copy(xgT[:, r % 2, :], psX[r % 2][:, 0:SLOTS]).then_inc(xgT_ready, 1)
                n, r = k, m
                if inside(n):
                    act.wait_ge(hid_psum, n + 1)
                    wait(act, y_psum, n - 1)
                    for c in range(HC):
                        at = H + HC * D + c
                        nc.scalar.activation(hid[:, r % 2, c, :], psH[r % 2][:, c * SLOTS:(c + 1) * SLOTS], ACT.Relu,
                                             bias=wcur[:, r % 2, at:at + 1]).then_inc(hid_ready, 1)

            slot_tiles(act, tile_step, 1, 0)

        @block.vector
        def _(dve):
            dve.wait_ge(wload, 16 * N_WLOAD)
            dve.wait_ge(const_ready, 3)
            for n, col in enumerate((0, 2, 4)):
                last = dve.tensor_scalar(brep[:, n, :], ones[:, :], bcol[:, col:col + 1], None, ALU.mult)
            last.then_inc(setup_own, 1)
            for b in range(2):
                for h in range(GB):
                    dve.tensor_scalar(bsb[:, b, h, 0:W], ones[:, 0:W], bcol[:, 3:4], None, ALU.mult)
            dve.wait_ge(pe_setup, 1)
            dve.tensor_copy(wT[:, :, :], psT[:, :].rearrange("p (n d) -> p n d", n=4)).then_inc(setup_own, 1)
            dve.wait_ge(pe_setup, 2)
            dve.tensor_copy(wqk[:, :], psA[:, 0:D])
            dve.tensor_copy(wvo[:, :], psA[:, D:2 * D])
            dve.tensor_scalar(wloc[:, :], psA[:, 2 * D:3 * D], 0.5 / W, None, ALU.mult)
            dve.tensor_copy(qbias[:, :], psB[:, 0:1])
            dve.tensor_copy(wgate[:, E:E + 1], psB[:, 2:3])
            dve.tensor_scalar(qkb[:, :], psB[:, 4:5], SCALE, None, ALU.mult)
            dve.tensor_tensor(b2r[:, :], psB[0:TG * E, D:2 * D], b2r[:, :], ALU.add).then_inc(setup_own, 1)
            dve.wait_ge(setup_own, 3)
            dve.tensor_tensor(b2r[:, :], b2r[:, :], bor[:, :], ALU.add).then_inc(setup_done, 1)

            def blocks(j):
                return j // 2, (slice(0, P) if j % 2 == 0 else slice(P, 3 * P))

            def table():
                own = 0

                def link(ins):
                    nonlocal own
                    own += 1
                    ins.then_inc(table_own, 1)
                    dve.wait_ge(table_own, own)

                dve.tensor_copy(basei[:, :], base[:, :]).then_inc(table_ready, 1)
                link(dve.tensor_tensor(cnt[:, :], base[:, :], lbase[:, :], ALU.subtract))
                link(dve.tensor_scalar(cnti[:, :], cnt[:, :], float(SLOTS - 1), None, ALU.add))
                link(dve.tensor_scalar(cnti[:, :], cnti[:, :], SLOTS.bit_length() - 1, None, ALU.logical_shift_right))
                link(dve.tensor_copy(ntile[:, :], cnti[:, :]))
                link(dve.tensor_copy(ends[:, 0, :], ntile[:, :]))
                for n in range(3):
                    link(dve.tensor_copy(ends[:, n + 1, :], ends[:, n, :]))
                    d = 1 << n
                    link(dve.tensor_tensor(ends[:, n + 1, d:E], ends[:, n, d:E], ends[:, n, 0:E - d], ALU.add))
                link(dve.tensor_tensor(begin[:, :], ends[:, 3, :], ntile[:, :], ALU.subtract))
                link(dve.tensor_tensor(chosen[:, 0, :], begin[:, :], kth[:, :], ALU.is_le))
                link(dve.tensor_tensor(chosen[:, 1, :], ends[:, 3, :], kth[:, :], ALU.is_le))
                link(dve.tensor_tensor(chosen[:, 0, :], chosen[:, 0, :], chosen[:, 1, :], ALU.subtract))
                link(dve.tensor_tensor(cnt[:, :], kth[:, :], begin[:, :], ALU.subtract))
                link(dve.tensor_scalar(cnt[:, :], cnt[:, :], float(SLOTS), -float(E * LIST), ALU.mult, ALU.add))
                link(dve.tensor_tensor(cnt[:, :], cnt[:, :], lbase[:, :], ALU.add))
                link(dve.tensor_tensor(chosen[:, 1, :], chosen[:, 0, :], cnt[:, :], ALU.mult))
                link(dve.tensor_tensor(chosen[:, 2, :], chosen[:, 0, :], lane[:, 0, :], ALU.mult))
                link(dve.tensor_reduce(sched[:, 1:2], chosen[:, 1, :], AX_X, ALU.add))
                link(dve.tensor_reduce(sched[:, 0:1], chosen[:, 2, :], AX_X, ALU.add))
                link(dve.tensor_scalar(sched[:, 1:2], sched[:, 1:2], float(E * LIST), None, ALU.add))
                assert own == TABLE_STEPS, own

            def table_out():
                dve.wait_ge(table_psum, 1)
                dve.tensor_copy(schedi[:, :, :], psG[0:1, 0:2 * P].rearrange("p (n k) -> p n k", n=2)
                                ).then_inc(table_ready, 1)

            def step(t, par):
                g, b = group(t, par, 2)
                if g is not None:
                    dve.wait_ge(a_psum, g + 1)
                    dve.wait_ge(b_ready, g + 1)
                    wait(dve, hsum_ready, g)
                    a = psA[:, :].rearrange("p (h n) -> p h n", h=GB)
                    for w in range(W):
                        last = dve.tensor_tensor(u[:, w, :, :], a, bsb[:, b, :, W - 1 - w:W - 1 - w + N], ALU.add)
                    last.then_inc(u_ready, 1)
                    dve.wait_ge(gate_psum, g + 1)
                    dve.tensor_copy(lg[:, :, :], psG[:, LOGITS:LOGITS + TG * 16].rearrange(
                        "p (j e) -> p j e", j=TG)[:, :, 0:E + 1]).then_inc(gate_read, 1)
                    dve.wait_ge(gate_read, g + 1)
                    dve.tensor_scalar(cb[:, b, :], lg[:, :, E], SCALE, qkb[:, :], ALU.mult, ALU.add).then_inc(cb_ready, 1)
                    for j in range(TG):
                        last = dve.max(gtop[:, j, :], lg[:, j, 0:E])
                    last.then_inc(gtop_ready, 1)
                    dve.wait_ge(gtop_ready, g + 1)
                    dve.tensor_tensor(gd[:, :], gtop[:, :, 0], gtop[:, :, 1], ALU.subtract).then_inc(gd_ready, 1)
                    for j in range(TG):
                        last = dve.max_index(gidx[:, j, :], gtop[:, j, :], lg[:, j, 0:E])
                    last.then_inc(gidx_ready, 1)
                    dve.wait_ge(gidx_ready, g + 1)
                    dve.tensor_copy(gif[:, :, :], gidx[:, :, 0:K]).then_inc(gif_ready, 1)
                    dve.wait_ge(gif_ready, g + 1)
                    wait(dve, row_ready, 2 * (g - 1))
                    dve.tensor_tensor(hot[:, b, :, :, :], lane[:, :, :].unsqueeze(1).to_broadcast([P, K, TG, E]),
                                      gif[:, :, :].rearrange("p j k -> p k j").unsqueeze(3).to_broadcast([P, K, TG, E]),
                                      ALU.is_equal).then_inc(hot_ready, 1)
                    dve.wait_ge(hot_ready, g + 1)
                    dve.tensor_tensor(both[:, b, :, :], hot[:, b, 0, :, :], hot[:, b, 1, :, :],
                                      ALU.add).then_inc(both_ready, 1)
                g, b = group(t, par, 1)
                if g is not None:
                    dve.wait_ge(rstd_ready, g + 1)
                    wait(dve, xT_psum, g - 1)
                    wait(dve, sent[b], halves(g - 2, b, 16 * K * TG) if not isinstance(g, int) or g >= 2 else 0)
                    for j in range(TG):
                        last = dve.tensor_scalar(rows[:, b, j, 0:D], tile(x, g, j),
                                                 mv[:, b, j, 0:1], rstd[:, b, j:j + 1], ALU.subtract, ALU.mult)
                    last.then_inc(xn_ready, 1)
                g, b = group(t, par, 0)
                if g is not None:
                    dve.wait_ge(xload[b], halves(g, b, 16))
                    for j in range(TG):
                        last = dve.bn_stats(st[:, b, j, :], tile(x, g, j))
                    last.then_inc(bn_ready, 1)
                    wait_small(dve, bn_ready, g + 1)
                    for j in range(TG):
                        last = dve.bn_aggr(mv[:, b, j, :], st[:, b, j, :])
                    last.then_inc(stats_ready, 1)
                g, b = group(t, par, 2)
                if g is not None:
                    dve.wait_ge(tanh_ready, g + 1)
                    dve.scalar_tensor_tensor(out=th[:, :, :, :].rearrange("p w h n -> p (w h n)"),
                                             in0=th[:, :, :, :].rearrange("p w h n -> p (w h n)"), scalar=1.0,
                                             in1=u[:, :, :, :].rearrange("p w h n -> p (w h n)"),
                                             op0=ALU.add, op1=ALU.mult).then_inc(prod_ready, 1)
                    dve.wait_ge(gth_ready, g + 1)
                    wait(dve, row_ready, 2 * g)
                    dve.tensor_scalar(gs[:, 0, :], gth[:, :], 0.5, 0.5, ALU.mult, ALU.add)
                    dve.tensor_scalar(gs[:, 1, :], gth[:, :], -0.5, 0.5, ALU.mult, ALU.add).then_inc(gs_ready, 1)
                    dve.wait_ge(prod_ready, 2 * g + 1)
                    half = W // 2
                    dve.tensor_tensor(th[:, 0:half, :, :], th[:, 0:half, :, :], th[:, half:W, :, :],
                                      ALU.add).then_inc(prod_ready, 1)
                    dve.wait_ge(prod_ready, 2 * g + 2)
                    wait(dve, loc_psum, g - 1)
                    dve.tensor_tensor(hsum[:, b, :].rearrange("p (h n) -> p h n", h=GB), th[:, 0, :, :], th[:, 1, :, :],
                                      ALU.add).then_inc(hsum_ready, 1)
                g, b = group(t, par, 3)
                if g is not None:
                    dve.wait_ge(loc_psum, g + 1)
                    dve.tensor_tensor(tiles(x, g), psQL[:, :].rearrange("p (j d) -> p j d", j=TG), tiles(x, g),
                                      ALU.add).then_inc(loc_read, 1)
                    dve.wait_ge(o_psum, g + 1)
                    dve.wait_ge(loc_read, g + 1)
                    for j in range(TG):
                        xj = tile(x, g, j)
                        last = dve.scalar_tensor_tensor(out=xj, in0=psVO[:, j * P:(j + 1) * P],
                                                        scalar=rden[:, b, j:j + 1], in1=xj, op0=ALU.mult, op1=ALU.add)
                    last.then_inc(out_read, 1)
                g, b = group(t, par, 2)
                if g is not None:
                    dve.wait_ge(rank_psum, g + 1)
                    wait(dve, place_ready, 2 * g)
                    dve.tensor_tensor(place[:, :, :], psG[:, RANK:RANK + TG * E].rearrange("p (j e) -> p j e", j=TG),
                                      base[:, :].unsqueeze(1).to_broadcast([P, TG, E]), ALU.add).then_inc(place_ready, 1)
                    dve.wait_ge(place_ready, 2 * g + 1)
                    dve.tensor_tensor(base[:, :], psG[:, TOTAL:TOTAL + E], base[:, :], ALU.add).then_inc(place_ready, 1)
                    dve.tensor_tensor(placed[:, :, :, :], hot[:, b, :, :, :],
                                      place[:, :, :].unsqueeze(1).to_broadcast([P, K, TG, E]),
                                      ALU.mult).then_inc(placed_ready, 1)
                    dve.wait_ge(placed_ready, g + 1)
                    dve.tensor_reduce(slotf[:, :, :], placed[:, :, :, :], AX_X, ALU.add).then_inc(slotf_ready, 1)
                    dve.wait_ge(slotf_ready, g + 1)
                    wait(dve, sent[b], halves(g - 2, b, 16 * K * TG) if not isinstance(g, int) or g >= 2 else 0)
                    dve.tensor_copy(slot[:, b, :, :], slotf[:, :, :]).then_inc(slot_ready, 1)
                    if isinstance(t, int) and t == NG + 1:
                        dve.wait_ge(place_ready, 2 * NG)
                        table()
                    wait_small(dve, s_ready, g + 1)
                    for j in range(TG):
                        h, at = blocks(j)
                        last = dve.max(top[:, j, :], s[:, h, at])
                    last.then_inc(max_ready, 1)
                    dve.wait_ge(max_ready, g + 1)
                    dve.tensor_scalar(negm[:, :], top[:, :, 0], -1.0, None, ALU.mult).then_inc(negm_ready, 1)
                    dve.tensor_tensor(topd[:, :, :], top[:, :, :], top[:, :, 0:1].to_broadcast([P, TG, TOP]),
                                      ALU.subtract).then_inc(topd_ready, 1)
                    for j in range(TG):
                        h, at = blocks(j)
                        last = dve.match_replace(rest[:, h, at], top[:, j, :], s[:, h, at], TAKEN)
                    last.then_inc(rest_ready, 1)
                    if isinstance(t, int) and t == NG + 1:
                        table_out()
                    dve.wait_ge(e_ready, g + 1)
                    dve.wait_ge(rest_ready, g + 1)
                    wait(dve, pT_psum, g)
                    dve.scalar_tensor_tensor(out=pr[:, :, :].rearrange("p h n -> p (h n)"),
                                             in0=rest[:, :, :].rearrange("p h n -> p (h n)"), scalar=TAKEN_BELOW,
                                             in1=e[:, :, :].rearrange("p h n -> p (h n)"),
                                             op0=ALU.is_le, op1=ALU.mult).then_inc(pr_ready, 1)
                    dve.wait_ge(tope_ready, g + 1)
                    dve.tensor_reduce(den[:, b, :], tope[:, :, :], AX_X, ALU.add).then_inc(den_ready, 1)
                    dve.wait_ge(den_ready, g + 1)
                    dve.reciprocal(rden[:, b, :], den[:, b, :]).then_inc(rden_ready, 1)

            run_steps(dve, step)

            dve.wait_ge(eload, 16 * (1 + 2 * HC))
            dve.wait_ge(table_ready, 2)

            def y_out(n, r):
                dve.wait_ge(y_psum, n + 1)
                if not isinstance(n, int) or n >= 2:
                    dve.wait_ge(returned[r % 2], halves(n - 2, r % 2, 16 * JS))
                for j in range(JS):
                    last = dve.tensor_scalar(y[:, r % 2, j, :], psY[r % 2][:, j * P:(j + 1) * P],
                                             gsc[:, r % XB, j:j + 1], None, ALU.mult)
                last.then_inc(y_ready, 1)

            def weights(n, r, expert):
                wait(dve, y_psum, n - 1)
                dve.tensor_copy(wcur[:, r % 2, :], wexp[:, bass.ds(expert, 1), :].rearrange("p a d -> p (a d)")
                                ).then_inc(wcur_ready, 1)
                dve.wait_ge(gathered[r % XB], passes(n, r))
                if not isinstance(n, int) or n >= XB:
                    dve.wait_ge(returned[r % 2], halves(n - XB, r % 2, 16 * JS))
                dve.tensor_copy(gsc[:, r % XB, :], xg[:, r % XB, :, bass.ds(expert + D, 1)].rearrange("p j a -> p (j a)"))
                dve.tensor_copy(gto[:, r % XB, :], xg[:, r % XB, :, bass.ds(expert + (D + E), 1)].rearrange(
                    "p j a -> p (j a)")).then_inc(gto_ready, 1)

            def round_of(k0):
                experts = nc.values_load_multi_w_load_instructions(
                    schedi[0:1, 0, bass.ds(k0, UN)], engines=(mybir.EngineType.DVE,), min_val=0, max_val=E - 1,
                    skip_runtime_bounds_check_because="the schedule names the E experts only")[1]
                for m in range(UN):
                    weights(k0 + m, m, experts[m])
                    if not isinstance(k0, int) or m >= 2:
                        y_out(k0 + (m - 2), (m - 2) % UN)

            round_of(0)
            with dve.Fori(1, NS // UN) as n:
                round_of(n * UN)
            y_out(NS - 2, UN - 2)
            y_out(NS - 1, UN - 1)

            def add(g, b):
                dve.wait_ge(yload[b], K * passes(g, b))
                wait(dve, y_added, g)
                dve.tensor_tensor(tiles(x, g), tiles(x, g), yin[:, b, 0, :, :], ALU.add).then_inc(sum_ready, 1)
                dve.wait_ge(sum_ready, g + 1)
                dve.tensor_tensor(tiles(x, g), tiles(x, g), yin[:, b, 1, :, :], ALU.add).then_inc(y_added, 1)

            for g in range(4):
                add(g, g)
            with dve.Fori(1, NG // 4) as n:
                for k in range(4):
                    add(n * 4 + k, k)


_INS = ["L0_attn_mu", "L0_attn_Wq", "L0_attn_bq", "L0_attn_Wk", "L0_attn_bk", "L0_attn_Wv", "L0_attn_bv",
        "L0_attn_Wm1", "L0_attn_bm1", "L0_attn_Wm2", "L0_attn_bm2", "L0_attn_Wo", "L0_attn_bo",
        "L0_ffn_Wg", "L0_ffn_W1", "L0_ffn_b1", "L0_ffn_W2", "L0_ffn_b2"]


def kernel(**inputs):
    import numpy as _np
    import concourse.bacc as _bacc
    from concourse import mybir as _mybir
    from concourse.bass_utils import run_bass_kernel_spmd as _run

    nc = _bacc.Bacc("TRN2", target_bir_lowering=False, num_devices=1)
    arrays, args = {}, []
    for name in _INS:
        a = _np.ascontiguousarray(inputs[name])
        arrays[f"in_{name}"] = a
        args.append(nc.dram_tensor(f"in_{name}", a.shape, _mybir.dt.from_np(a.dtype), kind="ExternalInput").ap())
    shape = inputs["L0_attn_mu"].shape
    out = nc.dram_tensor("out_0", shape, _mybir.dt.float32, kind="ExternalOutput").ap()
    program(nc, *args, out)
    r = _run(nc, [arrays], core_ids=[0])
    return r.results[0]["out_0"]
```

```python
from contextlib import ExitStack

import concourse.bass as bass
from concourse import mybir

ALU = mybir.AluOpType
ACT = mybir.ActivationFunctionType
AX_X = mybir.AxisListType.X
F32 = mybir.dt.float32
BF16 = mybir.dt.bfloat16
U32 = mybir.dt.uint32

P = 128
TG = 4
W = 4
TOP = 8
K = 2
EPS = 1e-5
MASKED = -1e30
TAKEN = -3e38
TAKEN_BELOW = -1e37
JS = 2
UN = 8
RB = 4
XB = 8
YB = 4


def program(nc, mu, Wq, bq, Wk, bk, Wv, bv, Wm1, bm1, Wm2, bm2, Wo, bo, Wg, W1, b1, W2, b2, out):
    B, N, D = mu.shape
    E, _, H = W1.shape
    T = B * N
    NT = T // P
    NG = NT // TG
    GT = TG * P
    GB = GT // N
    HC = H // P
    SLOTS = JS * P
    NS = (K * T + E * (SLOTS - 1)) // SLOTS
    NS = -(-NS // UN) * UN
    LIST = T + SLOTS
    ROW = D + 2 * E
    NOWHERE = float(K * T)
    WX = H + HC * D + HC
    assert D == P and N == 2 * P and GB == 2 and HC == 2 and E == 8 and W == 4
    SCALE = float(D) ** -0.5
    SW = N // P + 1

    x_dram = mu.rearrange("b (j p) d -> p (b j) d", p=P)
    out_dram = out.rearrange("b (j p) d -> p (b j) d", p=P)
    lists = nc.dram_tensor("lists", [E * LIST + SLOTS, ROW], F32, kind="Internal").ap()
    results = nc.dram_tensor("results", [K * T, D], F32, kind="Internal").ap()
    results_by_tile = results.rearrange("(k t p) d -> p k t d", p=P, k=K)

    with ExitStack() as ctx:
        def sb(name, shape, dt=F32):
            return ctx.enter_context(nc.sbuf_tensor(name, shape, dt))

        def sem(name):
            return ctx.enter_context(nc.semaphore(name))

        x = sb("x", [P, NT, D])
        wq, wk, wv, wm2 = (sb(n, [P, D]) for n in ("wq", "wk", "wv", "wm2"))
        wm1 = sb("wm1", [P, 2, D])
        wo = sb("wo", [P, 2, D])
        wT = sb("wT", [P, 4, D])
        wqk = sb("wqk", [P, D])
        wvo = sb("wvo", [P, D])
        wloc = sb("wloc", [P, D])
        wgate = sb("wgate", [P, E + 1])
        wexp = sb("wexp", [P, E, WX])
        bcol = sb("bcol", [P, 5])
        brep = sb("brep", [P, 3, P])
        qbias = sb("qbias", [P, 1])
        qkb = sb("qkb", [P, 1])
        b2r = sb("b2r", [TG * E, D])
        bor = sb("bor", [TG * E, D])
        b2blk = sb("b2blk", [TG * E, TG, D])
        ident = sb("ident", [P, P])
        identb = sb("identb", [P, P], BF16)
        future = sb("future", [P, P], BF16)
        earlier = sb("earlier", [P, P], BF16)
        onesb = sb("onesb", [P, P], BF16)
        ones = sb("ones", [P, P])
        lane = sb("lane", [P, TG, E])
        power = sb("power", [P, 3, TG])
        second = sb("second", [P, TG, E])
        gstep = sb("gstep", [P, TG])
        tok = sb("tok", [P, TG])
        scratch = sb("scratch", [P, 2])
        idle = sb("idle", [P, 1])
        st = sb("st", [P, 2, TG, 6])
        mv = sb("mv", [P, 2, TG, 2])
        rstd = sb("rstd", [P, 2, TG])
        shift = sb("shift", [P, 2, TG])
        rows = sb("rows", [P, RB, TG, ROW])
        xt = sb("xt", [P, 2, GT])
        bsb = sb("bsb", [P, 2, GB, W + N])
        u = sb("u", [P, W, GB, N])
        silu = sb("silu", [P, W, GB, N])
        part = sb("part", [P, GT])
        pairs = sb("pairs", [P, W // 2, GT])
        q = sb("q", [P, 2, GT])
        v = sb("v", [P, 2, TG, D])
        s = sb("s", [P, GB, SW * P])
        rest = sb("rest", [P, 2, GB, SW * P])
        e = sb("e", [P, GB, SW * P])
        pr = sb("pr", [P, GB, SW * P])
        pT = sb("pT", [P, GB, SW * P])
        top = sb("top", [P, TG, TOP])
        negm = sb("negm", [P, TG])
        topd = sb("topd", [P, TG, TOP])
        tope = sb("tope", [P, TG, TOP])
        den = sb("den", [P, TG])
        rden = sb("rden", [P, 2, TG])
        lg = sb("lg", [P, TG, E + 1])
        cb = sb("cb", [P, TG])
        gtop = sb("gtop", [P, TG, 8])
        gidx = sb("gidx", [P, TG, 8], U32)
        gif = sb("gif", [P, TG, K])
        hot = sb("hot", [P, 2, K, TG, E])
        both = sb("both", [P, TG, E], BF16)
        gd = sb("gd", [P, TG])
        gth = sb("gth", [P, TG])
        gs = sb("gs", [P, K, TG])
        gw = sb("gw", [P, K, TG, E])
        weight = sb("weight", [P, TG, E])
        gdst = sb("gdst", [P, TG, E])
        base = sb("base", [P, E])
        place = sb("place", [P, TG, E])
        placed = sb("placed", [P, K, TG, E])
        slotf = sb("slotf", [P, K, TG])
        slot = sb("slot", [P, 2, K, TG], U32)
        scT = sb("scT", [TG * E, 2, P])
        pad = sb("pad", [P, JS, ROW])
        lbase = sb("lbase", [P, E])
        cnt = sb("cnt", [P, E])
        cnti = sb("cnti", [P, E], U32)
        ntile = sb("ntile", [P, E])
        ends = sb("ends", [P, 4, E])
        begin = sb("begin", [P, E])
        kth = sb("kth", [P, E])
        chosen = sb("chosen", [P, 3, E])
        sched = sb("sched", [P, 2])
        schedi = sb("schedi", [1, 2, P], U32)
        basei = sb("basei", [P, E], U32)
        xg = sb("xg", [P, XB, JS, ROW])
        xgT = sb("xgT", [P, 2, SLOTS])
        wcur = sb("wcur", [P, YB, WX])
        hid = sb("hid", [P, 2, HC, SLOTS])
        gsc = sb("gsc", [P, XB, JS])
        gto = sb("gto", [P, XB, JS], U32)
        y = sb("y", [P, YB, JS, D])
        yin = sb("yin", [P, 4, K, TG, D])

        ps = [ctx.enter_context(nc.psum_tensor(f"ps{i}", [P, 512], F32)) for i in range(8)]
        psXB, psA, psQV, psL, psO = ps[0:5]
        psS = [ps[5], ps[6]]
        psG = ps[7]
        LOGITS, SCT, RANK, TOTAL = 0, P, 2 * P, 2 * P + TG * E
        psX, psH, psY = ps[0:2], ps[2:4], ps[4:6]

        tload = sem("tload")
        wload = sem("wload")
        mload = sem("mload")
        eload = sem("eload")
        xload = [sem("xload0"), sem("xload1")]
        const_ready = sem("const_ready")
        late_const = sem("late_const")
        pe_setup = sem("pe_setup")
        setup_own = sem("setup_own")
        setup_done = sem("setup_done")
        pool_own = sem("pool_own")
        stats_ready = sem("stats_ready")
        var_ready = sem("var_ready")
        rstd_ready = sem("rstd_ready")
        shift_ready = sem("shift_ready")
        xn_ready = sem("xn_ready")
        xn_dve_ready = sem("xn_dve_ready")
        xT_psum = sem("xT_psum")
        xT_ready = sem("xT_ready")
        gate_psum = sem("gate_psum")
        a_psum = sem("a_psum")
        b_psum = sem("b_psum")
        q_psum = sem("q_psum")
        v_psum = sem("v_psum")
        s_psum = sem("s_psum")
        pT_psum = sem("pT_psum")
        scT_psum = sem("scT_psum")
        rank_psum = sem("rank_psum")
        loc_psum = sem("loc_psum")
        o_psum = sem("o_psum")
        b_ready = sem("b_ready")
        q_ready = sem("q_ready")
        v_ready = sem("v_ready")
        s_ready = sem("s_ready")
        e_ready = sem("e_ready")
        tope_ready = sem("tope_ready")
        gth_ready = sem("gth_ready")
        pT_ready = sem("pT_ready")
        scT_ready = sem("scT_ready")
        silu_ready = sem("silu_ready")
        gate_read = sem("gate_read")
        cb_ready = sem("cb_ready")
        gtop_ready = sem("gtop_ready")
        gidx_ready = sem("gidx_ready")
        gif_ready = sem("gif_ready")
        hot_ready = sem("hot_ready")
        both_ready = sem("both_ready")
        gd_ready = sem("gd_ready")
        gs_ready = sem("gs_ready")
        place_ready = sem("place_ready")
        placed_ready = sem("placed_ready")
        slotf_ready = sem("slotf_ready")
        slot_ready = sem("slot_ready")
        gw_ready = sem("gw_ready")
        row_ready = sem("row_ready")
        tok_ready = sem("tok_ready")
        sent = [sem(f"sent{i}") for i in range(RB)]
        u_ready = sem("u_ready")
        pairs_ready = sem("pairs_ready")
        bn_ready = sem("bn_ready")
        max_ready = sem("max_ready")
        negm_ready = sem("negm_ready")
        topd_ready = sem("topd_ready")
        pr_ready = sem("pr_ready")
        den_ready = sem("den_ready")
        rest_ready = sem("rest_ready")
        sum_ready = sem("sum_ready")
        rden_ready = sem("rden_ready")
        part_ready = sem("part_ready")
        out_read = sem("out_read")
        table_own = sem("table_own")
        table_psum = sem("table_psum")
        table_ready = sem("table_ready")
        padded = sem("padded")
        gathered = [sem(f"gathered{i}") for i in range(XB)]
        xgT_psum = sem("xgT_psum")
        xgT_ready = sem("xgT_ready")
        wcur_ready = sem("wcur_ready")
        gto_ready = sem("gto_ready")
        hid_psum = sem("hid_psum")
        hid_ready = sem("hid_ready")
        y_psum = sem("y_psum")
        y_ready = sem("y_ready")
        returned = [sem(f"returned{i}") for i in range(YB)]
        yload = [sem(f"yload{i}") for i in range(4)]
        y_added = sem("y_added")
        stored = sem("stored")
        idled = sem("idled")

        block = ctx.enter_context(nc.Block())

        LAGS = 3
        NORM_ACT = TG - 2
        N_TLOAD = 4
        N_WLOAD = 1 + 4
        N_MLOAD = 3 + 1 + TG
        TABLE_STEPS = 23

        def wait(eng, sm, n):
            if isinstance(n, int) and n <= 0:
                return
            eng.wait_ge(sm, n)

        def wait_small(eng, sm, n, at=0):
            wait(eng, sm, n)
            eng.memset(scratch[:, at:at + 1], 0.0)

        def run_steps(eng, body):
            lo = LAGS + 2
            hi = lo + (NG - lo) // RB * RB
            for t in range(lo):
                body(t, t % RB)
            with eng.Fori(0, (hi - lo) // RB) as n:
                for k in range(RB):
                    body(n * RB + (lo + k), (lo + k) % RB)
            for t in range(hi, NG + LAGS):
                body(t, t % RB)

        def group(t, par, lag):
            if isinstance(t, int) and not 0 <= t - lag < NG:
                return None, None
            return t - lag, (par - lag) % RB

        def early(t, steps):
            return isinstance(t, int) and t < steps

        def until(n):
            return min(n, NG) if isinstance(n, int) else n

        def wait_sent(eng, g, b, back):
            if isinstance(g, int) and g < back:
                return
            past = (b - back) % RB
            per_group = 16 * K * TG
            if isinstance(g, int):
                eng.wait_ge(sent[past], ((g - back) // RB + 1) * per_group)
            else:
                eng.wait_ge(sent[past], (g + (RB - back - past)) * (per_group // RB))

        def blocks(j):
            return j // 2, (slice(0, P) if j % 2 == 0 else slice(P, SW * P))

        def tiles(tensor, g):
            return tensor[:, bass.ds(g * TG, TG), :]

        def tile(tensor, g, j):
            return tensor[:, bass.ds(g * TG + j, 1), :].rearrange("p a d -> p (a d)")

        def halves(g, b, per_group):
            return (g // 2 + 1) * per_group if isinstance(g, int) else (g + (2 - b)) * (per_group // 2)

        def passes(n, r, nb, each=16):
            return each * (n // nb + 1) if isinstance(n, int) else (n + (nb - r % nb)) * (each // nb)

        def slot_tiles(eng, body, lead, lag):
            for k in range(-lead, UN):
                body(k)
            with eng.Fori(1, NS // UN - 1) as n:
                for k in range(UN):
                    body(n * UN + k, k)
            for k in range(NS - UN, NS + lag):
                body(k)

        @block.sync
        def _(sp):
            def load(g, b):
                wait(sp, xload[b], 16 * (g // 2) if isinstance(g, int) else (g - b) * 8)
                sp.dma_start(tiles(x, g), tiles(x_dram, g)).then_inc(xload[b], 16)

            load(0, 0)
            for dst, src in ((wq, Wq), (wk, Wk), (wv, Wv), (wm2, Wm2)):
                sp.dma_start(dst[:, :], src).then_inc(tload, 16)
            sp.dma_start(wo[:, :, :], Wo.rearrange("(a p) d -> p a d", p=P)).then_inc(wload, 16)
            for n, src in ((0, bq), (1, bk), (2, bv), (4, bm2)):
                sp.dma_start(bcol[:, n:n + 1], src.rearrange("(p a) -> p a", a=1)).then_inc(wload, 16)
            load(1, 1)
            sp.dma_start(bcol[:, 3:4], bm1.rearrange("(p a) -> p a", a=1)).then_inc(mload, 16)
            for n in range(TG):
                sp.dma_start(b2r[n * E:(n + 1) * E, :], b2).then_inc(mload, 16)
            sp.dma_start(wm1[:, :, :], Wm1.rearrange("(a p) d -> p a d", p=P)).then_inc(mload, 16)
            sp.dma_start(wgate[:, 0:E], Wg).then_inc(mload, 16)
            sp.dma_start(bor[:, :], bo.rearrange("(a d) -> a d", a=1).to_broadcast([TG * E, D])).then_inc(mload, 16)
            sp.dma_start(wexp[:, :, 0:H], W1.rearrange("e d h -> d e h")).then_inc(eload, 16)
            for c in range(HC):
                sp.dma_start(wexp[:, :, H + c * D:H + (c + 1) * D],
                             W2[:, c * P:(c + 1) * P, :].rearrange("e p d -> p e d")).then_inc(eload, 16)
            for c in range(HC):
                sp.dma_start(wexp[:, :, H + HC * D + c:H + HC * D + c + 1],
                             b1[:, c * P:(c + 1) * P].rearrange("e (p a) -> p e a", a=1),
                             allow_slow_non_contiguous=True).then_inc(eload, 16)
            with sp.Fori(1, NG // 2) as n:
                for k in range(2):
                    load(n * 2 + k, k)

            sp.wait_ge(late_const, 2)
            sp.dma_start(lists[E * LIST:E * LIST + SLOTS, :].rearrange("(j p) d -> p j d", p=P),
                         pad[:, :, :]).then_inc(padded, 16)
            sp.wait_ge(table_ready, 1)
            starts = nc.values_load_multi_w_load_instructions(
                basei[0:1, :], engines=(mybir.EngineType.SP,), min_val=0, max_val=E * LIST - SLOTS,
                skip_runtime_bounds_check_because="a list holds at most T rows")[1]
            for start in starts:
                sp.dma_start(lists[bass.ds(start, SLOTS), :].rearrange("(j p) d -> p j d", p=P),
                             pad[:, :, :]).then_inc(padded, 16)
            sp.wait_ge(table_ready, 2)

            def fetch(k0, first):
                rows_of = nc.values_load_multi_w_load_instructions(
                    schedi[0:1, 1, bass.ds(k0, UN)], engines=(mybir.EngineType.SP,), min_val=0, max_val=E * LIST,
                    skip_runtime_bounds_check_because="the schedule names rows of the lists only")[1]
                if first:
                    for sm in sent:
                        sp.wait_ge(sm, 16 * K * TG * NG // RB)
                    sp.wait_ge(padded, 16 * (E + 1))
                for k in range(UN):
                    if not (first and k < XB):
                        sp.wait_ge(xgT_psum, k0 + k - XB + 1)
                        sp.wait_ge(gto_ready, k0 + k - XB + 1)
                    sp.dma_start(xg[:, k % XB, :, :],
                                 lists[bass.ds(rows_of[k], SLOTS), :].rearrange("(j p) d -> p j d", p=P)
                                 ).then_inc(gathered[k % XB], 16)

            fetch(0, True)
            with sp.Fori(1, NS // UN) as n:
                fetch(n * UN, False)

            for sm in returned:
                sp.wait_ge(sm, 16 * JS * NS // YB)

            def bring(g, b):
                wait(sp, y_added, g - 3)
                for k in range(K):
                    sp.dma_start(yin[:, b, k, :, :], results_by_tile[:, k, bass.ds(g * TG, TG), :]).then_inc(yload[b], 16)

            def store(g):
                sp.wait_ge(y_added, g + 1)
                sp.dma_start(tiles(out_dram, g), tiles(x, g)).then_inc(stored, 16)

            for g in range(4):
                bring(g, g % 4)
            with sp.Fori(1, NG // 4) as n:
                for k in range(4):
                    store(n * 4 + (k - 4))
                    bring(n * 4 + k, k)
            for g in range(NG - 4, NG):
                store(g)
            sp.wait_ge(stored, 16 * NG)

        @block.gpsimd
        def _(pool):
            own = 0

            def link(ins):
                nonlocal own
                own += 1
                ins.then_inc(pool_own, 1)
                pool.wait_ge(pool_own, own)

            link(pool.memset(ones[:, :], 1.0))
            pool.affine_select(out=ident[:, :], in_=ones[:, :], compare_op=ALU.is_equal, fill=0.0, base=0,
                               pattern=[[-1, P]], channel_multiplier=1).then_inc(const_ready, 1)
            pool.memset(power[:, 0, :], -0.5)
            pool.memset(power[:, 2, :], -1.0)
            pool.memset(power[:, 1, :], EPS).then_inc(const_ready, 1)
            link(pool.iota(lane[:, :, :], [[0, TG], [1, E]], base=0, channel_multiplier=0,
                           allow_small_or_imprecise_dtypes=True))
            link(pool.memset(onesb[:, :], 1.0))
            link(pool.affine_select(out=identb[:, :], in_=onesb[:, :], compare_op=ALU.is_equal, fill=0.0, base=0,
                                    pattern=[[-1, P]], channel_multiplier=1))
            link(pool.affine_select(out=earlier[:, :], in_=onesb[:, :], compare_op=ALU.is_ge, fill=0.0, base=-1,
                                    pattern=[[1, P]], channel_multiplier=-1))
            link(pool.memset(future[:, :], 0.0))
            link(pool.affine_select(out=future[:, :], in_=future[:, :], compare_op=ALU.is_ge, fill=MASKED, base=0,
                                    pattern=[[-1, P]], channel_multiplier=1))
            link(pool.memset(second[:, :, :], float(T)))
            link(pool.memset(gstep[:, :], float(GT)))
            link(pool.iota(tok[:, :], [[P, TG]], base=0, channel_multiplier=1,
                           allow_small_or_imprecise_dtypes=True))
            link(pool.iota(kth[:, :], [[0, E]], base=0, channel_multiplier=1,
                           allow_small_or_imprecise_dtypes=True))
            link(pool.iota(lbase[:, :], [[LIST, E]], base=0, channel_multiplier=0,
                           allow_small_or_imprecise_dtypes=True))
            pool.iota(base[:, :], [[LIST, E]], base=0, channel_multiplier=0,
                      allow_small_or_imprecise_dtypes=True).then_inc(const_ready, 1)
            def normal(g, b):
                pool.wait_ge(stats_ready, g + 1)
                wait(pool, xn_ready, g - 1)
                wait(pool, xn_dve_ready, g - 1)
                pool.tensor_tensor(rstd[:, b % 2, :], mv[:, b % 2, :, 1], power[:, 1, :], ALU.add)
                pool.tensor_tensor(shift[:, b % 2, :], mv[:, b % 2, :, 0], power[:, 2, :],
                                   ALU.mult).then_inc(var_ready, 1)
                pool.wait_ge(var_ready, g + 1)
                pool.tensor_tensor(rstd[:, b % 2, :], rstd[:, b % 2, :], power[:, 0, :],
                                   ALU.pow).then_inc(rstd_ready, 1)
                pool.wait_ge(rstd_ready, g + 1)
                pool.tensor_tensor(shift[:, b % 2, :], shift[:, b % 2, :], rstd[:, b % 2, :],
                                   ALU.mult).then_inc(shift_ready, 1)

            normal(0, 0)
            normal(1, 1)

            pool.wait_ge(setup_done, 1)
            for n in range(TG):
                last = pool.tensor_copy(b2blk[:, n, :], b2r[:, :])
            link(last)
            link(pool.affine_select(out=b2blk[:, :, :], in_=b2blk[:, :, :], compare_op=ALU.is_ge, fill=0.0, base=0,
                                    pattern=[[-E, TG], [0, D]], channel_multiplier=1))
            pool.affine_select(out=b2blk[:, :, :], in_=b2blk[:, :, :], compare_op=ALU.is_ge, fill=0.0, base=E - 1,
                               pattern=[[E, TG], [0, D]], channel_multiplier=-1).then_inc(late_const, 1)
            link(pool.memset(pad[:, :, :], 0.0))
            pool.memset(pad[:, :, D + E:ROW], NOWHERE).then_inc(late_const, 1)

            def step(t, par):
                g, b = group(t, par, 0)
                if g is not None and not early(t, 2):
                    normal(g, b)
                g, b = group(t, par, 1)
                if g is not None:
                    pool.wait_ge(gs_ready, g + 1)
                    wait(pool, row_ready, 2 * g)
                    pool.tensor_tensor(gw[:, :, :, :], hot[:, b % 2, :, :, :],
                                       gs[:, :, :].unsqueeze(3).to_broadcast([P, K, TG, E]),
                                       ALU.mult).then_inc(gw_ready, 1)
                    pool.tensor_tensor(gdst[:, :, :], hot[:, b % 2, 1, :, :], second[:, :, :],
                                       ALU.mult).then_inc(gw_ready, 1)
                    wait(pool, tok_ready, g)
                    wait(pool, scT_psum, g)
                    wait_sent(pool, g, b, RB)
                    pool.wait_ge(gw_ready, 2 * g + 2)
                    pool.tensor_tensor(weight[:, :, :], gw[:, 0, :, :], gw[:, 1, :, :], ALU.add)
                    pool.tensor_tensor(rows[:, b, :, D:D + E], gw[:, 0, :, :], gw[:, 1, :, :],
                                       ALU.add).then_inc(row_ready, 1)
                    pool.tensor_tensor(rows[:, b, :, D + E:ROW], gdst[:, :, :],
                                       tok[:, :].unsqueeze(2).to_broadcast([P, TG, E]), ALU.add).then_inc(row_ready, 1)
                    pool.wait_ge(row_ready, 2 * g + 2)
                    pool.tensor_tensor(tok[:, :], tok[:, :], gstep[:, :], ALU.add).then_inc(tok_ready, 1)
                g, b = group(t, par, 2)
                if g is not None:
                    wait(pool, idled, g)
                    pool.wait_ge(slot_ready, g + 1)
                    pool.tensor_tensor(idle[:, :], ones[:, 0:1], ones[:, 0:1], ALU.mult).then_inc(idled, 1)
                    for k in range(K):
                        for j in range(TG):
                            pool.indirect_dma_start(lists,
                                                    bass.IndirectOffsetOnAxis(ap=slot[:, b % 2, k, j:j + 1], axis=0),
                                                    rows[:, b, j, :], None).then_inc(sent[b], 16)

            run_steps(pool, step)

            def await_y(tiles_done, waited):
                pool.wait_ge(idled, NG + waited)
                pool.wait_ge(y_ready, tiles_done)
                pool.tensor_tensor(idle[:, :], ones[:, 0:1], ones[:, 0:1], ALU.mult).then_inc(idled, 1)

            def give(m):
                for j in range(JS):
                    pool.indirect_dma_start(results, bass.IndirectOffsetOnAxis(ap=gto[:, m % XB, j:j + 1], axis=0),
                                            y[:, m % YB, j, :], None, bounds_check=K * T - 1,
                                            oob_is_err=False).then_inc(returned[m % YB], 16)

            for m in range(UN):
                await_y(m + 1, m)
                give(m)
            with pool.Fori(1, NS // UN) as n:
                for m in range(UN):
                    if m % 2 == 0:
                        await_y(n * UN + (m + 2), n * (UN // 2) + (UN // 2 + m // 2))
                    give(m)

        @block.tensor
        def _(pe):
            def neighbours(g, b):
                pe.wait_ge(xT_ready, g + 1)
                pe.matmul(psXB[:, :], wm1[:, 1, :], xt[:, b % 2, :], start=True, stop=True).then_inc(b_psum, 1)

            def turn(g, b):
                pe.wait_ge(xn_ready, g + 1)
                pe.wait_ge(xn_dve_ready, g + 1)
                wait(pe, b_ready, g)
                for j in range(TG):
                    last = pe.transpose(psXB[:, j * P:(j + 1) * P], rows[:, b, j, 0:D], ident[:, :])
                last.then_inc(xT_psum, 1)

            pe.wait_ge(const_ready, 1)
            pe.wait_ge(tload, 16 * N_TLOAD)
            for n, w in enumerate((wq, wk, wv, wm2)):
                last = pe.transpose(psL[:, n * P:(n + 1) * P], w[:, :], ident[:, :])
            last.then_inc(pe_setup, 1)
            turn(0, 0)
            pe.wait_ge(setup_own, 2)
            pe.wait_ge(wload, 16 * N_WLOAD)
            pe.matmul(psA[:, 0:D], wT[:, 0, :], wT[:, 1, :], start=True, stop=True)
            pe.matmul(psA[:, D:2 * D], wT[:, 2, :], wo[:, 1, :], start=True, stop=True)
            pe.matmul(psA[:, 2 * D:3 * D], wT[:, 3, :], wo[:, 0, :], start=True, stop=True)
            pe.matmul(psQV[:, 0:1], wT[:, 1, :], bcol[:, 0:1], start=True, stop=True)
            pe.matmul(psQV[:, 2:3], wT[:, 0, :], bcol[:, 1:2], start=True, stop=True)
            pe.matmul(psQV[:, 4:5], brep[:, 0, :], bcol[:, 1:2], start=True, stop=True)
            pe.matmul(psQV[0:TG * E, D:2 * D], brep[:, 1, 0:TG * E], wo[:, 1, :], start=True, stop=False)
            pe.matmul(psQV[0:TG * E, D:2 * D], brep[:, 2, 0:TG * E], wo[:, 0, :], start=False,
                      stop=True).then_inc(pe_setup, 1)
            pe.wait_ge(mload, 16 * N_MLOAD)
            neighbours(0, 0)
            pe.wait_ge(setup_done, 1)
            pe.wait_ge(const_ready, 3)

            def step(t, par):
                if isinstance(t, int) and t == NG + 2:
                    pe.wait_ge(table_own, TABLE_STEPS)
                    pe.wait_ge(place_ready, 2 * NG)
                    for n in range(2):
                        last = pe.transpose(psG[0:1, n * P:(n + 1) * P], sched[:, n:n + 1], ident[:, :])
                    last.then_inc(table_psum, 1)
                g, b = group(t, par, 3)
                if g is not None:
                    wait(pe, out_read, g)
                    pe.matmul(psL[:, :], ident[:, :], tiles(x, g), start=True, stop=False, skip_group_check=True)
                    pe.wait_ge(pairs_ready, g + 1)
                    for w in range(W // 2):
                        for j in range(TG):
                            pe.matmul(psL[:, j * P:(j + 1) * P], pairs[:, w, j * P:(j + 1) * P], wloc[:, :],
                                      start=False, stop=False, skip_group_check=True)
                    pe.wait_ge(late_const, 1)
                    pe.wait_ge(scT_ready, g + 1)
                    pe.matmul(psL[:, :], scT[:, b % 2, :], b2blk[:, :, :], start=False, stop=True,
                              skip_group_check=True).then_inc(loc_psum, 1)
                    pe.wait_ge(pT_ready, g + 1)
                    pe.wait_ge(v_ready, g + 1)
                    for h in range(GB):
                        o = psO[:, 2 * h * P:(2 * h + 1) * P]
                        pe.matmul(o, pT[:, h, 0:P], v[:, b % 2, 2 * h, :], start=True, stop=True)
                        o = psO[:, (2 * h + 1) * P:(2 * h + 2) * P]
                        pe.matmul(o, pT[:, h, P:2 * P], v[:, b % 2, 2 * h, :], start=True, stop=False)
                        last = pe.matmul(o, pT[:, h, 2 * P:3 * P], v[:, b % 2, 2 * h + 1, :], start=False, stop=True)
                    last.then_inc(o_psum, 1)
                g, b = group(t, par, 0)
                if g is not None and not early(t, 1):
                    turn(g, b)
                g, b = group(t, par, 2)
                if g is not None:
                    pe.wait_ge(pr_ready, g + 1)
                    pe.wait_ge(s_ready, until(g + 2))
                    for h in range(GB):
                        for k in range(SW):
                            last = pe.transpose(psS[h][:, k * P:(k + 1) * P], pr[:, h, k * P:(k + 1) * P],
                                                ident[:, :])
                    last.then_inc(pT_psum, 1)
                g, b = group(t, par, 1)
                if g is not None:
                    pe.wait_ge(row_ready, 2 * g + 2)
                    wait(pe, place_ready, 2 * g)
                    pe.transpose(psG[0:TG * E, SCT:SCT + P], weight[:, :, :], ident[:, :]).then_inc(scT_psum, 1)
                g, b = group(t, par, 0)
                if g is not None:
                    xg_t = xt[:, b % 2, :]
                    pe.wait_ge(xT_ready, g + 1)
                    wait(pe, v_ready, g)
                    pe.matmul(psQV[:, :], wqk[:, :], xg_t, start=True, stop=True).then_inc(q_psum, 1)
                    if not early(t, 1):
                        neighbours(g, b)
                    wait(pe, u_ready, g)
                    pe.matmul(psA[:, :], wm1[:, 0, :], xg_t, start=True, stop=True).then_inc(a_psum, 1)
                    wait(pe, scT_ready, g)
                    for j in range(TG):
                        last = pe.matmul(psG[:, LOGITS + j * 16:LOGITS + j * 16 + E + 1],
                                         xt[:, b % 2, j * P:(j + 1) * P], wgate[:, :], start=True, stop=True)
                    last.then_inc(gate_psum, 1)
                    pe.wait_ge(q_ready, g + 1)
                    wait(pe, pT_ready, g - 1)
                    for h in range(GB):
                        k0, k1 = (xt[:, b % 2, (2 * h + k) * P:(2 * h + k + 1) * P] for k in range(2))
                        q0, q1 = (q[:, b % 2, (2 * h + k) * P:(2 * h + k + 1) * P] for k in range(2))
                        pe.matmul(psS[h][:, 0:P], q0, k0, start=True, stop=False)
                        pe.matmul(psS[h][:, 0:P], identb[:, :], future[:, :], start=False, stop=True)
                        pe.matmul(psS[h][:, P:2 * P], q1, k0, start=True, stop=True)
                        pe.matmul(psS[h][:, 2 * P:3 * P], q1, k1, start=True, stop=False)
                        last = pe.matmul(psS[h][:, 2 * P:3 * P], identb[:, :], future[:, :], start=False, stop=True)
                    last.then_inc(s_psum, 1)
                    for j in range(TG):
                        last = pe.matmul(psQV[:, j * P:(j + 1) * P], xt[:, b % 2, j * P:(j + 1) * P], wvo[:, :],
                                         start=True, stop=True)
                    last.then_inc(v_psum, 1)
                g, b = group(t, par, 1)
                if g is not None:
                    pe.wait_ge(both_ready, g + 1)
                    pe.wait_ge(gate_read, until(g + 2))
                    pe.wait_ge(scT_ready, g + 1)
                    rank = psG[:, RANK:RANK + TG * E]
                    pe.matmul(rank, earlier[:, :], both[:, :, :], start=True, stop=False)
                    for j in range(1, TG):
                        pe.matmul(psG[:, RANK + j * E:RANK + TG * E], onesb[:, :], both[:, 0:TG - j, :],
                                  start=False, stop=(j == TG - 1))
                    for j in range(TG):
                        last = pe.matmul(psG[:, TOTAL:TOTAL + E], onesb[:, :], both[:, j, :],
                                         start=(j == 0), stop=(j == TG - 1))
                    last.then_inc(rank_psum, 1)

            run_steps(pe, step)

            pe.wait_ge(xT_ready, NG)

            def tile_step(k, m=None):
                m = k % UN if m is None else m
                inside = lambda n: not isinstance(n, int) or 0 <= n < NS
                n, r = k + 1, (m + 1) % UN
                if inside(n):
                    pe.wait_ge(gathered[r % XB], passes(n, r, XB))
                    wait(pe, xgT_ready, n - 1)
                    for j in range(JS):
                        last = pe.transpose(psX[r % 2][:, j * P:(j + 1) * P], xg[:, r % XB, j, 0:D], ident[:, :])
                    last.then_inc(xgT_psum, 1)
                n, r = k, m
                if inside(n):
                    pe.wait_ge(xgT_ready, n + 1)
                    pe.wait_ge(wcur_ready, n + 1)
                    wait(pe, hid_ready, HC * (n - 1))
                    if isinstance(n, int) and n == 1:
                        pe.wait_ge(out_read, NG)
                    for c in range(HC):
                        last = pe.matmul(psH[r % 2][:, c * SLOTS:(c + 1) * SLOTS], wcur[:, r % YB, c * P:(c + 1) * P],
                                         xgT[:, r % 2, :], start=True, stop=True)
                    last.then_inc(hid_psum, 1)
                n, r = k - 1, (m - 1) % UN
                if inside(n):
                    pe.wait_ge(hid_ready, HC * (n + 1))
                    wait(pe, y_ready, n - 1)
                    for j in range(JS):
                        for c in range(HC):
                            last = pe.matmul(psY[r % 2][:, j * P:(j + 1) * P], hid[:, r % 2, c, j * P:(j + 1) * P],
                                             wcur[:, r % YB, H + c * D:H + (c + 1) * D], start=(c == 0),
                                             stop=(c == HC - 1))
                    last.then_inc(y_psum, 1)

            slot_tiles(pe, tile_step, 1, 1)

        @block.scalar
        def _(act):
            def layernorm(g, b):
                act.wait_ge(shift_ready, g + 1)
                wait_sent(act, g, b, RB)
                for j in range(NORM_ACT):
                    last = nc.scalar.activation(rows[:, b, j, 0:D], tile(x, g, j), ACT.Identity,
                                                scale=rstd[:, b % 2, j:j + 1], bias=shift[:, b % 2, j:j + 1])
                last.then_inc(xn_ready, 1)

            layernorm(0, 0)

            def step(t, par):
                g, b = group(t, par, 1)
                if g is not None:
                    act.wait_ge(gd_ready, g + 1)
                    wait(act, gs_ready, g)
                    nc.scalar.activation(gth[:, :], gd[:, :], ACT.Tanh, scale=0.5).then_inc(gth_ready, 1)
                g, b = group(t, par, 2)
                if g is not None:
                    act.wait_ge(u_ready, g + 1)
                    wait(act, pairs_ready, g)
                    nc.scalar.activation(silu[:, :, :, :], u[:, :, :, :], ACT.Silu).then_inc(silu_ready, 1)
                g, b = group(t, par, 0)
                if g is not None:
                    if not early(t, 2):
                        layernorm(g, b)
                g, b = group(t, par, 3)
                if g is not None:
                    act.wait_ge(loc_psum, g + 1)
                    wait(act, out_read, g)
                    nc.scalar.copy(part[:, :], psL[:, :]).then_inc(part_ready, 1)
                g, b = group(t, par, 1)
                if g is not None:
                    act.wait_ge(v_psum, g + 1)
                    wait(act, o_psum, g - 1)
                    nc.scalar.copy(v[:, b % 2, :, :], psQV[:, :].rearrange("p (j d) -> p j d", j=TG)
                                   ).then_inc(v_ready, 1)
                g, b = group(t, par, 0)
                if g is not None:
                    act.wait_ge(xT_psum, g + 1)
                    wait(act, s_psum, g - 1)
                    nc.scalar.copy(xt[:, b % 2, :], psXB[:, :]).then_inc(xT_ready, 1)
                    if early(t, 1):
                        layernorm(1, 1)
                g, b = group(t, par, 2)
                if g is not None:
                    act.wait_ge(pT_psum, g + 1)
                    wait(act, o_psum, g)
                    for h in range(GB):
                        last = nc.scalar.copy(pT[:, h, :], psS[h][:, 0:SW * P])
                    last.then_inc(pT_ready, 1)
                g, b = group(t, par, 1)
                if g is not None:
                    act.wait_ge(scT_psum, g + 1)
                    wait(act, loc_psum, g - 1)
                    nc.scalar.copy(scT[:, b % 2, :], psG[0:TG * E, SCT:SCT + P]).then_inc(scT_ready, 1)
                g, b = group(t, par, 0)
                if g is not None:
                    act.wait_ge(q_psum, g + 1)
                    act.wait_ge(setup_done, 1)
                    wait(act, s_psum, g - 1)
                    nc.scalar.activation(q[:, b % 2, :], psQV[:, :], ACT.Identity, bias=qbias[:, :]
                                         ).then_inc(q_ready, 1)
                    act.wait_ge(b_psum, g + 1)
                    wait(act, u_ready, g - 1)
                    nc.scalar.activation(bsb[:, b % 2, :, W:W + N], psXB[:, :].rearrange("p (h n) -> p h n", h=GB),
                                         ACT.Identity, bias=bcol[:, 3:4]).then_inc(b_ready, 1)
                g, b = group(t, par, 1)
                if g is not None:
                    act.wait_ge(negm_ready, g + 1)
                    wait(act, pr_ready, g)
                    for j in range(TG):
                        h, at = blocks(j)
                        last = nc.scalar.activation(e[:, h, at], s[:, h, at], ACT.Exp, bias=negm[:, j:j + 1])
                    last.then_inc(e_ready, 1)
                    act.wait_ge(topd_ready, g + 1)
                    wait(act, den_ready, g)
                    nc.scalar.activation(tope[:, :, :], topd[:, :, :], ACT.Exp).then_inc(tope_ready, 1)
                g, b = group(t, par, 0)
                if g is not None:
                    act.wait_ge(s_psum, g + 1)
                    act.wait_ge(cb_ready, g + 1)
                    wait(act, rest_ready, g)
                    wait(act, e_ready, g)
                    for j in range(TG):
                        h, at = blocks(j)
                        last = nc.scalar.activation(s[:, h, at], psS[h][:, at], ACT.Identity, scale=SCALE,
                                                    bias=cb[:, j:j + 1])
                    last.then_inc(s_ready, 1)

            run_steps(act, step)

            def tile_step(k, m=None):
                m = k % UN if m is None else m
                inside = lambda n: not isinstance(n, int) or 0 <= n < NS
                n, r = k + 1, (m + 1) % UN
                if inside(n):
                    act.wait_ge(xgT_psum, n + 1)
                    wait(act, hid_psum, n - 1)
                    nc.scalar.copy(xgT[:, r % 2, :], psX[r % 2][:, 0:SLOTS]).then_inc(xgT_ready, 1)
                n, r = k, m
                if inside(n):
                    act.wait_ge(hid_psum, n + 1)
                    wait(act, y_psum, n - 1)
                    for c in range(HC):
                        at = H + HC * D + c
                        nc.scalar.activation(hid[:, r % 2, c, :], psH[r % 2][:, c * SLOTS:(c + 1) * SLOTS], ACT.Relu,
                                             bias=wcur[:, r % YB, at:at + 1]).then_inc(hid_ready, 1)

            slot_tiles(act, tile_step, 1, 0)

        @block.vector
        def _(dve):
            def statistics(g, b):
                dve.wait_ge(xload[b % 2], halves(g, b % 2, 16))
                wait(dve, stats_ready, g - 1)
                for j in range(TG):
                    last = dve.bn_stats(st[:, b % 2, j, :], tile(x, g, j))
                last.then_inc(bn_ready, 1)

            def normalise(g, b):
                dve.wait_ge(shift_ready, g + 1)
                wait_sent(dve, g, b, RB)
                for j in range(NORM_ACT, TG):
                    last = dve.tensor_scalar(rows[:, b, j, 0:D], tile(x, g, j), rstd[:, b % 2, j:j + 1],
                                             shift[:, b % 2, j:j + 1], ALU.mult, ALU.add)
                last.then_inc(xn_dve_ready, 1)

            def moments(g, b):
                wait(dve, shift_ready, g - 1)
                wait_small(dve, bn_ready, g + 1)
                for j in range(TG):
                    last = dve.bn_aggr(mv[:, b % 2, j, :], st[:, b % 2, j, :])
                last.then_inc(stats_ready, 1)

            statistics(0, 0)
            moments(0, 0)
            normalise(0, 0)
            dve.wait_ge(pe_setup, 1)
            dve.tensor_copy(wT[:, :, :], psL[:, :].rearrange("p (n d) -> p n d", n=4)).then_inc(setup_own, 1)
            dve.wait_ge(wload, 16 * N_WLOAD)
            dve.wait_ge(const_ready, 3)
            for n, col in enumerate((0, 2, 4)):
                last = dve.tensor_scalar(brep[:, n, :], ones[:, :], bcol[:, col:col + 1], None, ALU.mult)
            last.then_inc(setup_own, 1)
            statistics(1, 1)
            moments(1, 1)
            normalise(1, 1)
            dve.wait_ge(mload, 16 * N_MLOAD)
            for b in range(2):
                for h in range(GB):
                    dve.tensor_scalar(bsb[:, b, h, 0:W], ones[:, 0:W], bcol[:, 3:4], None, ALU.mult)
            dve.wait_ge(pe_setup, 2)
            dve.tensor_copy(wqk[:, :], psA[:, 0:D])
            dve.tensor_copy(wvo[:, :], psA[:, D:2 * D])
            dve.tensor_scalar(wloc[:, :], psA[:, 2 * D:3 * D], 1.0 / W, None, ALU.mult)
            dve.tensor_copy(qbias[:, :], psQV[:, 0:1])
            dve.tensor_copy(wgate[:, E:E + 1], psQV[:, 2:3])
            dve.tensor_scalar(qkb[:, :], psQV[:, 4:5], SCALE, None, ALU.mult)
            dve.tensor_tensor(b2r[:, :], psQV[0:TG * E, D:2 * D], b2r[:, :], ALU.add).then_inc(setup_own, 1)
            dve.wait_ge(setup_own, 3)
            dve.tensor_tensor(b2r[:, :], b2r[:, :], bor[:, :], ALU.add).then_inc(setup_done, 1)

            def table():
                own = 0

                def link(ins):
                    nonlocal own
                    own += 1
                    ins.then_inc(table_own, 1)
                    dve.wait_ge(table_own, own)

                dve.tensor_copy(basei[:, :], base[:, :]).then_inc(table_ready, 1)
                link(dve.tensor_tensor(cnt[:, :], base[:, :], lbase[:, :], ALU.subtract))
                link(dve.tensor_scalar(cnti[:, :], cnt[:, :], float(SLOTS - 1), None, ALU.add))
                link(dve.tensor_scalar(cnti[:, :], cnti[:, :], SLOTS.bit_length() - 1, None, ALU.logical_shift_right))
                link(dve.tensor_copy(ntile[:, :], cnti[:, :]))
                link(dve.tensor_copy(ends[:, 0, :], ntile[:, :]))
                for n in range(3):
                    link(dve.tensor_copy(ends[:, n + 1, :], ends[:, n, :]))
                    d = 1 << n
                    link(dve.tensor_tensor(ends[:, n + 1, d:E], ends[:, n, d:E], ends[:, n, 0:E - d], ALU.add))
                link(dve.tensor_tensor(begin[:, :], ends[:, 3, :], ntile[:, :], ALU.subtract))
                link(dve.tensor_tensor(chosen[:, 0, :], begin[:, :], kth[:, :], ALU.is_le))
                link(dve.tensor_tensor(chosen[:, 1, :], ends[:, 3, :], kth[:, :], ALU.is_le))
                link(dve.tensor_tensor(chosen[:, 0, :], chosen[:, 0, :], chosen[:, 1, :], ALU.subtract))
                link(dve.tensor_tensor(cnt[:, :], kth[:, :], begin[:, :], ALU.subtract))
                link(dve.tensor_scalar(cnt[:, :], cnt[:, :], float(SLOTS), -float(E * LIST), ALU.mult, ALU.add))
                link(dve.tensor_tensor(cnt[:, :], cnt[:, :], lbase[:, :], ALU.add))
                link(dve.tensor_tensor(chosen[:, 1, :], chosen[:, 0, :], cnt[:, :], ALU.mult))
                link(dve.tensor_tensor(chosen[:, 2, :], chosen[:, 0, :], lane[:, 0, :], ALU.mult))
                link(dve.tensor_reduce(sched[:, 1:2], chosen[:, 1, :], AX_X, ALU.add))
                link(dve.tensor_reduce(sched[:, 0:1], chosen[:, 2, :], AX_X, ALU.add))
                link(dve.tensor_scalar(sched[:, 1:2], sched[:, 1:2], float(E * LIST), None, ALU.add))
                assert own == TABLE_STEPS, own

            def step(t, par):
                g, b = group(t, par, 0)
                if g is not None and not early(t, 2):
                    statistics(g, b)
                g, b = group(t, par, 2)
                if g is not None:
                    dve.wait_ge(rank_psum, g + 1)
                    wait(dve, place_ready, 2 * g)
                    wait(dve, placed_ready, g)
                    dve.tensor_tensor(place[:, :, :], psG[:, RANK:RANK + TG * E].rearrange("p (j e) -> p j e", j=TG),
                                      base[:, :].unsqueeze(1).to_broadcast([P, TG, E]), ALU.add).then_inc(place_ready, 1)
                    dve.wait_ge(place_ready, 2 * g + 1)
                    dve.tensor_tensor(base[:, :], psG[:, TOTAL:TOTAL + E], base[:, :], ALU.add).then_inc(place_ready, 1)
                g, b = group(t, par, 1)
                if g is not None:
                    dve.wait_ge(gth_ready, g + 1)
                    wait(dve, gw_ready, 2 * g)
                    dve.tensor_scalar(gs[:, 0, :], gth[:, :], 0.5, 0.5, ALU.mult, ALU.add)
                    dve.tensor_scalar(gs[:, 1, :], gth[:, :], -0.5, 0.5, ALU.mult, ALU.add).then_inc(gs_ready, 1)
                g, b = group(t, par, 0)
                if g is not None and not early(t, 2):
                    moments(g, b)
                g, b = group(t, par, 1)
                if g is not None:
                    wait_small(dve, s_ready, g + 1, 1)
                    for j in range(TG):
                        h, at = blocks(j)
                        last = dve.max(top[:, j, :], s[:, h, at])
                    last.then_inc(max_ready, 1)
                g, b = group(t, par, 2)
                if g is not None:
                    wait(dve, slotf_ready, g)
                    dve.tensor_tensor(placed[:, :, :, :], hot[:, b % 2, :, :, :],
                                      place[:, :, :].unsqueeze(1).to_broadcast([P, K, TG, E]),
                                      ALU.mult).then_inc(placed_ready, 1)
                    dve.wait_ge(den_ready, g + 1)
                    wait(dve, out_read, g - 1)
                    dve.reciprocal(rden[:, b % 2, :], den[:, :]).then_inc(rden_ready, 1)
                g, b = group(t, par, 1)
                if g is not None:
                    dve.wait_ge(max_ready, g + 1)
                    wait(dve, e_ready, g)
                    dve.tensor_scalar(negm[:, :], top[:, :, 0], -1.0, None, ALU.mult).then_inc(negm_ready, 1)
                    wait(dve, tope_ready, g)
                    dve.tensor_tensor(topd[:, :, :], top[:, :, :], top[:, :, 0:1].to_broadcast([P, TG, TOP]),
                                      ALU.subtract).then_inc(topd_ready, 1)
                    for j in range(TG):
                        h, at = blocks(j)
                        last = dve.match_replace(rest[:, b % 2, h, at], top[:, j, :], s[:, h, at], TAKEN)
                    last.then_inc(rest_ready, 1)
                g, b = group(t, par, 0)
                if g is not None and not early(t, 2):
                    normalise(g, b)
                g, b = group(t, par, 2)
                if g is not None:
                    dve.wait_ge(placed_ready, g + 1)
                    wait(dve, slot_ready, g)
                    dve.tensor_reduce(slotf[:, :, :], placed[:, :, :, :], AX_X, ALU.add).then_inc(slotf_ready, 1)
                    dve.wait_ge(e_ready, g + 1)
                    dve.wait_ge(rest_ready, g + 1)
                    wait(dve, pT_psum, g)
                    dve.scalar_tensor_tensor(out=pr[:, :, :].rearrange("p h n -> p (h n)"),
                                             in0=rest[:, b % 2, :, :].rearrange("p h n -> p (h n)"),
                                             scalar=TAKEN_BELOW, in1=e[:, :, :].rearrange("p h n -> p (h n)"),
                                             op0=ALU.is_le, op1=ALU.mult).then_inc(pr_ready, 1)
                    dve.wait_ge(slotf_ready, g + 1)
                    wait_sent(dve, g, b, 2)
                    dve.tensor_copy(slot[:, b % 2, :, :], slotf[:, :, :]).then_inc(slot_ready, 1)
                if isinstance(t, int) and t == NG + 1:
                    dve.wait_ge(place_ready, 2 * NG)
                    table()
                g, b = group(t, par, 1)
                if g is not None:
                    dve.wait_ge(a_psum, g + 1)
                    dve.wait_ge(b_ready, g + 1)
                    wait(dve, silu_ready, g)
                    a = psA[:, :].rearrange("p (h n) -> p h n", h=GB)
                    for w in range(W):
                        last = dve.tensor_tensor(u[:, w, :, :], a, bsb[:, b % 2, :, W - 1 - w:W - 1 - w + N], ALU.add)
                    last.then_inc(u_ready, 1)
                    dve.wait_ge(hot_ready, g + 1)
                    wait(dve, rank_psum, g)
                    dve.tensor_tensor(both[:, :, :], hot[:, b % 2, 0, :, :], hot[:, b % 2, 1, :, :],
                                      ALU.add).then_inc(both_ready, 1)
                g, b = group(t, par, 2)
                if g is not None:
                    dve.wait_ge(silu_ready, g + 1)
                    wait(dve, loc_psum, g)
                    dve.tensor_tensor(pairs[:, :, :].rearrange("p w (h n) -> p w h n", h=GB),
                                      silu[:, 0:W // 2, :, :], silu[:, W // 2:W, :, :], ALU.add
                                      ).then_inc(pairs_ready, 1)
                if isinstance(t, int) and t == NG + 2:
                    dve.wait_ge(table_psum, 1)
                    dve.tensor_copy(schedi[:, :, :], psG[0:1, 0:2 * P].rearrange("p (n k) -> p n k", n=2)
                                    ).then_inc(table_ready, 1)
                g, b = group(t, par, 3)
                if g is not None:
                    dve.wait_ge(part_ready, g + 1)
                    dve.wait_ge(o_psum, g + 1)
                    dve.wait_ge(rden_ready, g + 1)
                    for j in range(TG):
                        at = slice(j * P, (j + 1) * P)
                        last = dve.scalar_tensor_tensor(out=tile(x, g, j), in0=psO[:, at],
                                                        scalar=rden[:, b % 2, j:j + 1], in1=part[:, at],
                                                        op0=ALU.mult, op1=ALU.add)
                    last.then_inc(out_read, 1)
                g, b = group(t, par, 0)
                if g is not None:
                    dve.wait_ge(gate_psum, g + 1)
                    dve.tensor_copy(lg[:, :, :], psG[:, LOGITS:LOGITS + TG * 16].rearrange(
                        "p (j e) -> p j e", j=TG)[:, :, 0:E + 1]).then_inc(gate_read, 1)
                    wait(dve, s_ready, g)
                    dve.wait_ge(gate_read, g + 1)
                    dve.tensor_scalar(cb[:, :], lg[:, :, E], SCALE, qkb[:, :], ALU.mult, ALU.add).then_inc(cb_ready, 1)
                    for j in range(TG):
                        last = dve.max(gtop[:, j, :], lg[:, j, 0:E])
                    last.then_inc(gtop_ready, 1)
                    wait(dve, gth_ready, g)
                    dve.wait_ge(gtop_ready, g + 1)
                    dve.tensor_tensor(gd[:, :], gtop[:, :, 0], gtop[:, :, 1], ALU.subtract).then_inc(gd_ready, 1)
                    for j in range(TG):
                        last = dve.max_index(gidx[:, j, :], gtop[:, j, :], lg[:, j, 0:E])
                    last.then_inc(gidx_ready, 1)
                    dve.wait_ge(gidx_ready, g + 1)
                    dve.tensor_copy(gif[:, :, :], gidx[:, :, 0:K]).then_inc(gif_ready, 1)
                    dve.wait_ge(gif_ready, g + 1)
                    wait(dve, gw_ready, 2 * (g - 1))
                    dve.tensor_tensor(hot[:, b % 2, :, :, :], lane[:, :, :].unsqueeze(1).to_broadcast([P, K, TG, E]),
                                      gif[:, :, :].rearrange("p j k -> p k j").unsqueeze(3).to_broadcast([P, K, TG, E]),
                                      ALU.is_equal).then_inc(hot_ready, 1)
                g, b = group(t, par, 1)
                if g is not None:
                    wait(dve, rden_ready, g)
                    dve.wait_ge(tope_ready, g + 1)
                    dve.tensor_reduce(den[:, :], tope[:, :, :], AX_X, ALU.add).then_inc(den_ready, 1)

            run_steps(dve, step)

            dve.wait_ge(eload, 16 * (1 + 2 * HC))
            dve.wait_ge(table_ready, 2)

            def y_out(n, r):
                dve.wait_ge(y_psum, n + 1)
                if not isinstance(n, int) or n >= YB:
                    dve.wait_ge(returned[r % YB], passes(n - YB, r, YB, 16 * JS))
                for j in range(JS):
                    last = dve.tensor_scalar(y[:, r % YB, j, :], psY[r % 2][:, j * P:(j + 1) * P],
                                             gsc[:, r % XB, j:j + 1], None, ALU.mult)
                last.then_inc(y_ready, 1)

            def weights(n, r, expert):
                wait(dve, y_psum, n - YB + 1)
                dve.tensor_copy(wcur[:, r % YB, :], wexp[:, bass.ds(expert, 1), :].rearrange("p a d -> p (a d)")
                                ).then_inc(wcur_ready, 1)
                dve.wait_ge(gathered[r % XB], passes(n, r, XB))
                if not isinstance(n, int) or n >= XB:
                    dve.wait_ge(returned[r % YB], passes(n - XB, r, YB, 16 * JS))
                dve.tensor_copy(gsc[:, r % XB, :], xg[:, r % XB, :, bass.ds(expert + D, 1)].rearrange("p j a -> p (j a)"))
                dve.tensor_copy(gto[:, r % XB, :], xg[:, r % XB, :, bass.ds(expert + (D + E), 1)].rearrange(
                    "p j a -> p (j a)")).then_inc(gto_ready, 1)

            def round_of(k0):
                experts = nc.values_load_multi_w_load_instructions(
                    schedi[0:1, 0, bass.ds(k0, UN)], engines=(mybir.EngineType.DVE,), min_val=0, max_val=E - 1,
                    skip_runtime_bounds_check_because="the schedule names the E experts only")[1]
                for m in range(UN):
                    weights(k0 + m, m, experts[m])
                    if not isinstance(k0, int) or m >= 2:
                        y_out(k0 + (m - 2), (m - 2) % UN)

            round_of(0)
            with dve.Fori(1, NS // UN) as n:
                round_of(n * UN)
            y_out(NS - 2, UN - 2)
            y_out(NS - 1, UN - 1)

            def add(g, b):
                dve.wait_ge(yload[b], passes(g, b, 4, 16 * K))
                wait(dve, y_added, g)
                dve.tensor_tensor(tiles(x, g), tiles(x, g), yin[:, b, 0, :, :], ALU.add).then_inc(sum_ready, 1)
                dve.wait_ge(sum_ready, g + 1)
                dve.tensor_tensor(tiles(x, g), tiles(x, g), yin[:, b, 1, :, :], ALU.add).then_inc(y_added, 1)

            for g in range(4):
                add(g, g)
            with dve.Fori(1, NG // 4) as n:
                for k in range(4):
                    add(n * 4 + k, k)


_INS = ["L0_attn_mu", "L0_attn_Wq", "L0_attn_bq", "L0_attn_Wk", "L0_attn_bk", "L0_attn_Wv", "L0_attn_bv",
        "L0_attn_Wm1", "L0_attn_bm1", "L0_attn_Wm2", "L0_attn_bm2", "L0_attn_Wo", "L0_attn_bo",
        "L0_ffn_Wg", "L0_ffn_W1", "L0_ffn_b1", "L0_ffn_W2", "L0_ffn_b2"]


def kernel(**inputs):
    import numpy as _np
    import concourse.bacc as _bacc
    from concourse import mybir as _mybir
    from concourse.bass_utils import run_bass_kernel_spmd as _run

    nc = _bacc.Bacc("TRN2", target_bir_lowering=False, num_devices=1)
    arrays, args = {}, []
    for name in _INS:
        a = _np.ascontiguousarray(inputs[name])
        arrays[f"in_{name}"] = a
        args.append(nc.dram_tensor(f"in_{name}", a.shape, _mybir.dt.from_np(a.dtype), kind="ExternalInput").ap())
    shape = inputs["L0_attn_mu"].shape
    out = nc.dram_tensor("out_0", shape, _mybir.dt.float32, kind="ExternalOutput").ap()
    program(nc, *args, out)
    r = _run(nc, [arrays], core_ids=[0])
    return r.results[0]["out_0"]
```
